# Optimizing a Trainium2 kernel written in Bass

```python
import numpy as np
import jax
import jax.numpy as jnp

def _softmax(x, axis=-1):
    return jax.nn.softmax(x, axis=axis)

def _gelu(x):
    return jax.nn.gelu(x, approximate=True)

def _silu(x):
    return jax.nn.silu(x)

def _sigmoid(x):
    return jax.nn.sigmoid(x)

def _layernorm(x, axis=-1, eps=1e-05):
    m = jnp.mean(x, axis=axis, keepdims=True)
    v = jnp.var(x, axis=axis, keepdims=True)
    return (x - m) / jnp.sqrt(v + eps)

def _scatter_add(tgt, idx, src, axis=0):
    return tgt.at[idx].add(src)

def _segment_sum(src, seg, n):
    return jax.ops.segment_sum(src, seg, n)
kernel_name = 'mk_seq_preln_d1_jaxref_r4_927b5d'

def setup_inputs(seed: int=0):
    np.random.seed(seed)
    _w = jnp.asarray

    def _L0_attn_setup():
        import jax, jax.numpy as jnp
        import numpy as np
        B, S, D = (4, 512, 256)

        def _gaussian_mask(seq_len, dtype):
            pos = jnp.arange(seq_len, dtype=dtype)
            center = seq_len / 2
            sigma = seq_len / 4
            m = jnp.exp(-0.5 * ((pos - center) / sigma) ** 2)
            return m[None, None, :]
        key = jax.random.key(seed)
        ks = jax.random.split(key, 9)
        sc = 1.0 / np.sqrt(D)
        return {'x': jax.random.normal(ks[0], (B, S, D), dtype=jnp.float32), 'Wq': jax.random.normal(ks[1], (D, D), dtype=jnp.float32) * sc, 'bq': jnp.zeros((D,), dtype=jnp.float32), 'Wk': jax.random.normal(ks[2], (D, D), dtype=jnp.float32) * sc, 'bk': jnp.zeros((D,), dtype=jnp.float32), 'Wv': jax.random.normal(ks[3], (D, D), dtype=jnp.float32) * sc, 'bv': jnp.zeros((D,), dtype=jnp.float32), 'Wo': jax.random.normal(ks[4], (D, D), dtype=jnp.float32) * sc, 'bo': jnp.zeros((D,), dtype=jnp.float32)}
    _L0_attn_in = _L0_attn_setup()

    def _L0_ffn_setup():
        import jax, jax.numpy as jnp
        import numpy as np

        def _binarize(w):
            alpha = jax.lax.stop_gradient(jnp.mean(jnp.abs(w), axis=1, keepdims=True))
            bw = alpha * jnp.sign(w)
            return w + jax.lax.stop_gradient(bw - w)
        key = jax.random.key(seed)
        k1, k2, k3, k4, k5 = jax.random.split(key, 5)
        D, H = (256, 1024)
        x = jax.random.normal(k1, (64, 196, D), dtype=jnp.float32)
        w1 = jax.random.normal(k2, (H, D), dtype=jnp.float32) * 0.02
        b1 = jax.random.normal(k3, (H,), dtype=jnp.float32) * 0.02
        w2 = jax.random.normal(k4, (D, H), dtype=jnp.float32) * 0.02
        b2 = jax.random.normal(k5, (D,), dtype=jnp.float32) * 0.02
        return {'x': x, 'w1': w1, 'b1': b1, 'w2': w2, 'b2': b2}
    _L0_ffn_in = _L0_ffn_setup()
    _d = {'L0_attn_x': _L0_attn_in['x'], 'L0_attn_Wq': _L0_attn_in['Wq'], 'L0_attn_bq': _L0_attn_in['bq'], 'L0_attn_Wk': _L0_attn_in['Wk'], 'L0_attn_bk': _L0_attn_in['bk'], 'L0_attn_Wv': _L0_attn_in['Wv'], 'L0_attn_bv': _L0_attn_in['bv'], 'L0_attn_Wo': _L0_attn_in['Wo'], 'L0_attn_bo': _L0_attn_in['bo'], 'L0_ffn_w1': _L0_ffn_in['w1'], 'L0_ffn_b1': _L0_ffn_in['b1'], 'L0_ffn_w2': _L0_ffn_in['w2'], 'L0_ffn_b2': _L0_ffn_in['b2']}
    _x0 = _d['L0_attn_x']
    _d['L0_attn_x'] = jax.random.normal(jax.random.fold_in(jax.random.key(seed), 1), (16, 1024, 256), dtype=_x0.dtype)
    del _x0
    return _d

def reference(L0_attn_x, L0_attn_Wq, L0_attn_bq, L0_attn_Wk, L0_attn_bk, L0_attn_Wv, L0_attn_bv, L0_attn_Wo, L0_attn_bo, L0_ffn_w1, L0_ffn_b1, L0_ffn_w2, L0_ffn_b2):

    def _L0_attn_ref(x, Wq, bq, Wk, bk, Wv, bv, Wo, bo):
        import jax, jax.numpy as jnp
        import numpy as np
        B, S, D = (4, 512, 256)

        def _gaussian_mask(seq_len, dtype):
            pos = jnp.arange(seq_len, dtype=dtype)
            center = seq_len / 2
            sigma = seq_len / 4
            m = jnp.exp(-0.5 * ((pos - center) / sigma) ** 2)
            return m[None, None, :]
        d = x.shape[-1]
        Q = x @ Wq.T + bq
        K = x @ Wk.T + bk
        V = x @ Wv.T + bv
        scores = jnp.einsum('bqd,bkd->bqk', Q, K) / jnp.sqrt(jnp.asarray(d, x.dtype))
        scores = scores * _gaussian_mask(x.shape[1], x.dtype)
        attn = jax.nn.softmax(scores, axis=-1)
        out = jnp.einsum('bqk,bkd->bqd', attn, V)
        return out @ Wo.T + bo

    def _L0_ffn_ref(x, w1, b1, w2, b2):
        import jax, jax.numpy as jnp
        import numpy as np

        def _binarize(w):
            alpha = jax.lax.stop_gradient(jnp.mean(jnp.abs(w), axis=1, keepdims=True))
            bw = alpha * jnp.sign(w)
            return w + jax.lax.stop_gradient(bw - w)
        bw1 = _binarize(w1)
        h = jnp.einsum('bsd,hd->bsh', x, bw1) + b1
        h = jax.nn.gelu(h, approximate=False)
        bw2 = _binarize(w2)
        out = jnp.einsum('bsh,dh->bsd', h, bw2) + b2
        return out
    x = L0_attn_x
    x = x + _L0_attn_ref(_layernorm(x, axis=-1), L0_attn_Wq, L0_attn_bq, L0_attn_Wk, L0_attn_bk, L0_attn_Wv, L0_attn_bv, L0_attn_Wo, L0_attn_bo)
    x = x + _L0_ffn_ref(_layernorm(x, axis=-1), L0_ffn_w1, L0_ffn_b1, L0_ffn_w2, L0_ffn_b2)
    return x

_drawn_inputs = setup_inputs


def setup_inputs(seed=0):
    import zlib

    import numpy as np

    out = dict(_drawn_inputs(seed))
    spreads = {'L0_attn_bq': (0.0, 0.8),
     'L0_attn_bk': (0.0, 2.0),
     'L0_attn_bv': (0.0, 0.1),
     'L0_attn_bo': (0.0, 0.1)}
    factors = {'L0_ffn_b1': 8.0, 'L0_ffn_b2': 2.948}
    for name, (base, spread) in spreads.items():
        noise = np.random.default_rng([zlib.crc32(name.encode()), seed]).standard_normal(out[name].shape)
        drawn = base * np.exp(spread * noise) if base else spread * noise
        out[name] = jnp.asarray(drawn.astype(out[name].dtype))
    for name, factor in factors.items():
        out[name] = (out[name] * factor).astype(out[name].dtype)
    return out
```

```python
from contextlib import ExitStack

import numpy as np
import concourse.bass as bass
from concourse import mybir

F32 = mybir.dt.float32
F32R = mybir.dt.float32r
ACT = mybir.ActivationFunctionType
ALU = mybir.AluOpType
AX_X = mybir.AxisListType.X

P = 128
HALF = 512
EPS = 1e-5


def gaussian_mask_row(seq, tiles):
    pos = np.arange(seq, dtype=np.float32)
    mask = np.exp(np.float32(-0.5) * ((pos - np.float32(seq / 2)) / np.float32(seq / 4)) ** 2)
    return np.ascontiguousarray(mask.astype(np.float32).reshape(P, tiles).T).reshape(-1)


def preln_attention_ffn(nc, x, Wq, bq, Wk, bk, Wv, bv, Wo, bo, w1, b1, w2, b2, mask, out):
    B, S, D = x.shape
    H = w1.shape[0]
    T = S // P
    C = D // P
    J = H // P
    N2 = S // HALF
    TH = T // N2
    PAIRS = B // 2
    QG = C * N2
    VG = T // 2
    SCALE = float(D) ** -0.5

    x_v = x.rearrange("b (p t) d -> b p t d", t=T)
    out_v = out.rearrange("b (p t) d -> b p t d", t=T)

    with ExitStack() as ctx:
        def sb(name, shape, dt=F32, stack=ctx):
            return stack.enter_context(nc.sbuf_tensor(name, shape, dt))

        def sem(name):
            return ctx.enter_context(nc.semaphore(name))

        ident = sb("ident", [P, P])
        ones = sb("ones", [P, P])
        mask_bc = sb("mask_bc", [P, S])
        bias_bc = sb("bias_bc", [P, D])
        b2_bc = sb("b2_bc", [P, D])
        alpha2_bc = sb("alpha2_bc", [P, D])
        alpha1 = sb("alpha1", [P, J])
        alpha2 = sb("alpha2", [P, C])
        cols = sb("cols", [P, J + 3 * C])
        ccol = sb("ccol", [P, C])
        wkt = sb("wkt", [P, C])
        Mh = sb("Mh", [P, C, D], F32R)
        Ml = sb("Ml", [P, C, D], F32R)
        Nh = sb("Nh", [P, C, D], F32R)
        Nl = sb("Nl", [P, C, D], F32R)
        sgn1 = sb("sgn1", [P, C, H], F32R)
        sgn2 = sb("sgn2", [P, J, D], F32R)
        xin = [sb(f"xin{s}", [P, T, D]) for s in range(2)]
        kh = sb("kh", [P, C, S], F32R)
        kl = sb("kl", [P, C, S], F32R)
        qh = sb("qh", [P, C, S], F32R)
        ql = sb("ql", [P, C, S], F32R)
        vh = sb("vh", [P, T, D], F32R)
        vl = sb("vl", [P, T, D], F32R)
        g = sb("g", [P, 2, S])
        ys = sb("ys", [P, 2, D])
        mhalf = sb("mhalf", [P, T])
        eps = sb("eps", [P, T])
        st1 = sb("st1", [P, T, 6])
        mv1 = sb("mv1", [P, T, 2])
        ve1 = sb("ve1", [P, T])
        rstd1 = sb("rstd1", [P, T])
        st2 = sb("st2", [P, T, 6])
        mv2 = sb("mv2", [P, T, 2])
        ve2 = sb("ve2", [P, T])
        rstd2 = sb("rstd2", [P, T])
        nmax = sb("nmax", [P, T])
        rsum = sb("rsum", [P, T])
        rinv = sb("rinv", [P, T])

        with ExitStack() as place:
            xn1 = sb("xn1", [P, T, D], F32, place)
            xn2 = sb("xn2", [P, T, D], F32, place)
        with ExitStack() as place:
            x2h = sb("x2h", [P, C, S], F32R, place)
            x2l = sb("x2l", [P, C, S], F32R, place)
            with ExitStack() as inner:
                xh = sb("xh", [P, C, S], F32R, inner)
                xl = sb("xl", [P, C, S], F32R, inner)
                kmf = sb("kmf", [P, C, S], F32, inner)
                prob = sb("prob", [P, 2, S], F32, inner)
                pth = sb("pth", [P, 2, S], F32R, inner)
                ptl = sb("ptl", [P, 2, S], F32R, inner)
            with ExitStack() as inner:
                sb("gap", [P, 3 * C * S], F32, inner)
                wq = sb("wq", [P, C, D], F32, inner)
                wk = sb("wk", [P, C, D], F32, inner)
                wv = sb("wv", [P, C, D], F32, inner)
                wo = sb("wo", [P, C, D], F32, inner)
                wkc = sb("wkc", [P, C, D], F32, inner)
                woT = sb("woT", [P, C, D], F32, inner)
                w1s = sb("w1s", [P, J, D], F32, inner)
                w2s = sb("w2s", [P, C, H], F32, inner)
                neg = sb("neg", [P, J, D], F32, inner)
                rows = sb("rows", [J + 3 * C, P], F32, inner)
                bvb = sb("bvb", [P, C, P], F32, inner)
                diag = sb("diag", [P, C, P], F32, inner)
            gh = sb("gh", [P, J, S], F32R, place)
            gl = sb("gl", [P, J, S], F32R, place)

        ps = ctx.enter_context(nc.psum_tensor("ps", [P, 8, HALF], F32))
        PT_BANK, OUT_BANK = 4, 6

        x_loaded = [sem(f"x_loaded{s}") for s in range(2)]
        wqk_loaded, wvo_loaded, wff_loaded, small_loaded = (
            sem(n) for n in ("wqk_loaded", "wvo_loaded", "wff_loaded", "small_loaded"))
        consts_set, cols_turned, prep_pe, prep_dve, prep_act = (
            sem(n) for n in ("consts_set", "cols_turned", "prep_pe", "prep_dve", "prep_act"))
        y_stored = sem("y_stored")
        stats1, aggr1, vareps1, rstd1_set, xn1_set, xbias_added = (
            sem(n) for n in ("stats1", "aggr1", "vareps1", "rstd1_set", "xn1_set", "xbias_added"))
        x_turned, xh_set, xl_set, km_set, kh_set, kl_set = (
            sem(n) for n in ("x_turned", "xh_set", "xl_set", "km_set", "kh_set", "kl_set"))
        q_summed, qh_set, ql_set, v_summed, vh_set, vl_set = (
            sem(n) for n in ("q_summed", "qh_set", "ql_set", "v_summed", "vh_set", "vl_set"))
        scored, max_set, exp_set, p_turned, pth_set, ptl_set, rinv_set, pv_summed, x1_set = (
            sem(n) for n in ("scored", "max_set", "exp_set", "p_turned", "pth_set", "ptl_set", "rinv_set",
                             "pv_summed", "x1_set"))
        stats2, aggr2, vareps2, rstd2_set, xn2_set, b2_added = (
            sem(n) for n in ("stats2", "aggr2", "vareps2", "rstd2_set", "xn2_set", "b2_added"))
        x2_turned, x2h_set, x2l_set, hidden, gelu_set, gh_set, gl_set = (
            sem(n) for n in ("x2_turned", "x2h_set", "x2l_set", "hidden", "gelu_set", "gh_set", "gl_set"))
        ffn_summed, ffn_scaled, y_set = (sem(n) for n in ("ffn_summed", "ffn_scaled", "y_set"))

        block = ctx.enter_context(nc.Block())

        def slot(s):
            return ps[:, 2 * s:2 * s + 2, :]

        def two(ap):
            return ap.rearrange("p (a n) -> p a n", a=2)

        def half(n):
            return slice(n * HALF, (n + 1) * HALF)

        def tile(t):
            return slice(t * P, (t + 1) * P)


        @block.sync
        def _(sp):
            sp.dma_start(xin[0][:], x_v[0]).then_inc(x_loaded[0], 16)
            sp.dma_start(w1s[:], w1.rearrange("(j p) d -> p j d", p=P)).then_inc(wff_loaded, 16)
            sp.dma_start(w2s[:], w2.rearrange("(c p) h -> p c h", p=P)).then_inc(wff_loaded, 16)
            sp.dma_start(xin[1][:], x_v[1]).then_inc(x_loaded[1], 16)

            def store_and_load(i, s, more):
                b = 2 * i + s
                for n in range(N2):
                    sp.wait_ge(y_set, T * b + TH * (n + 1))
                    sp.dma_start(out_v[b, :, n * TH:(n + 1) * TH, :],
                                 xin[s][:, n * TH:(n + 1) * TH, :]).then_inc(y_stored, 16)
                if more:
                    sp.wait_ge(y_stored, 16 * N2 * (b + 1))
                    sp.dma_start(xin[s][:], x_v[b + 2]).then_inc(x_loaded[s], 16)

            with sp.Fori(0, PAIRS - 1) as i:
                store_and_load(i, 0, True)
                store_and_load(i, 1, True)
            store_and_load(PAIRS - 1, 0, False)
            store_and_load(PAIRS - 1, 1, False)
            sp.wait_ge(y_stored, 16 * N2 * B)

        @block.gpsimd
        def _(pool):
            pool.memset(ident[:], 0.0).then_inc(consts_set, 1)
            pool.memset(ones[:], 1.0).then_inc(consts_set, 1)
            pool.memset(mhalf[:], -0.5).then_inc(consts_set, 1)
            pool.memset(eps[:], EPS).then_inc(consts_set, 1)
            pool.wait_ge(consts_set, 4)
            pool.affine_select(out=ident[:], in_=ident[:], compare_op=ALU.not_equal, fill=1.0, base=0,
                               pattern=[[-1, P]], channel_multiplier=1).then_inc(consts_set, 1)

            def rstd_attention(b):
                pool.wait_ge(aggr1, T * (b + 1))
                pool.tensor_tensor(ve1[:], mv1[:, :, 1], eps[:], ALU.add).then_inc(vareps1, 1)
                pool.wait_ge(vareps1, b + 1)
                pool.tensor_tensor(rstd1[:], ve1[:], mhalf[:], ALU.pow).then_inc(rstd1_set, 1)

            def rstd_ffn(b, q):
                pool.wait_ge(aggr2, T * b + q + 1)
                pool.tensor_tensor(ve2[:, q:q + 1], mv2[:, q, 1:2], eps[:, q:q + 1], ALU.add).then_inc(vareps2, 1)
                pool.wait_ge(vareps2, T * b + q + 1)
                pool.tensor_tensor(rstd2[:, q:q + 1], ve2[:, q:q + 1], mhalf[:, q:q + 1],
                                   ALU.pow).then_inc(rstd2_set, 1)

            def split_keys(b):
                for n in range(N2):
                    pool.wait_ge(kh_set, N2 * b + n + 1)
                    pool.tensor_tensor(kl[:, :, half(n)], kmf[:, :, half(n)],
                                       kh[:, :, half(n)].bitcast(F32), ALU.subtract).then_inc(kl_set, 1)

            def add_bias(b, s, t):
                if t == 0:
                    pool.wait_ge(xn1_set, T * (b + 1))
                pool.tensor_tensor(xin[s][:, t, :], xin[s][:, t, :], bias_bc[:], ALU.add).then_inc(xbias_added, 1)

            rstd_attention(0)
            split_keys(0)
            pool.wait_ge(prep_dve, 10)
            for t in range(T):
                add_bias(0, 0, t)

            def batch(i, s, more):
                b = 2 * i + s
                for q in range(TH):
                    rstd_ffn(b, q)
                if more:
                    rstd_attention(b + 1)
                for q in range(TH, T):
                    rstd_ffn(b, q)
                if more:
                    split_keys(b + 1)
                for j in range(J):
                    if j == 0:
                        pool.wait_ge(xn2_set, T * (b + 1))
                    pool.tensor_tensor(xin[s][:, j, :], xin[s][:, j, :], b2_bc[:], ALU.add).then_inc(b2_added, 1)
                for t in range(T):
                    if t == 0:
                        pool.wait_ge(b2_added, T * (b + 1))
                    pool.wait_ge(ffn_scaled, T * b + t + 1)
                    pool.tensor_tensor(xin[s][:, t, :], xin[s][:, t, :], ys[:, t % 2, :], ALU.add).then_inc(y_set, 1)
                    if more:
                        add_bias(b + 1, 1 - s, t)

            with pool.Fori(0, PAIRS - 1) as i:
                batch(i, 0, True)
                batch(i, 1, True)
            batch(PAIRS - 1, 0, True)
            batch(PAIRS - 1, 1, False)

        @block.scalar
        def _(act):
            act.dma_start(wq[:], Wq.rearrange("(c p) d -> p c d", p=P)).then_inc(wqk_loaded, 16)
            act.dma_start(wk[:], Wk.rearrange("(c p) d -> p c d", p=P)).then_inc(wqk_loaded, 16)
            act.dma_start(wv[:], Wv.rearrange("(c p) d -> p c d", p=P)).then_inc(wvo_loaded, 16)
            act.dma_start(wo[:], Wo.rearrange("(c p) d -> p c d", p=P)).then_inc(wvo_loaded, 16)
            act.dma_start(rows[0:J, :], b1.rearrange("(j p) -> j p", p=P)).then_inc(small_loaded, 16)
            for n, b_dram in enumerate((bq, bk, bv)):
                act.dma_start(rows[J + C * n:J + C * (n + 1), :],
                              b_dram.rearrange("(c p) -> c p", p=P)).then_inc(small_loaded, 16)
            act.dma_start(mask_bc[:], mask.partition_broadcast(P)).then_inc(small_loaded, 16)
            act.dma_start(bias_bc[:], bo.partition_broadcast(P)).then_inc(small_loaded, 16)
            act.dma_start(b2_bc[:], b2.partition_broadcast(P)).then_inc(small_loaded, 16)

            act.wait_ge(prep_pe, 1)
            act.activation(Mh[:].rearrange("p c d -> p (c d)"), ps[:, 0, :], ACT.Copy, scale=SCALE).then_inc(prep_act, 1)
            act.wait_ge(prep_pe, 4)
            act.activation(Nh[:].rearrange("p c d -> p (c d)"), ps[:, 3, :], ACT.Copy).then_inc(prep_act, 1)

            def hi_rows(b, n):
                act.wait_ge(x_turned, N2 * b + n + 1)
                act.activation(xh[:, :, half(n)], slot(n), ACT.Copy).then_inc(xh_set, 1)

            def hi_queries(b):
                for k in range(QG):
                    n, m = divmod(k, C)
                    act.wait_ge(q_summed, QG * b + k + 1)
                    act.activation(qh[:, m, half(n)], ps[:, PT_BANK + k, :], ACT.Identity,
                                   bias=ccol[:, m:m + 1]).then_inc(qh_set, 1)

            def hi_values(b):
                for k in range(VG):
                    act.wait_ge(v_summed, VG * b + k + 1)
                    act.activation(vh[:, 2 * k:2 * k + 2, :], two(ps[:, PT_BANK + k, :]), ACT.Copy).then_inc(vh_set, 1)

            def hi_keys(b):
                for n in range(N2):
                    act.wait_ge(km_set, N2 * b + n + 1)
                    act.activation(kh[:, :, half(n)], kmf[:, :, half(n)], ACT.Copy).then_inc(kh_set, 1)

            act.wait_ge(prep_dve, 5)
            for n in range(N2):
                hi_rows(0, n)
            hi_queries(0)
            hi_keys(0)
            hi_values(0)

            def exponentials(b, q):
                act.wait_ge(max_set, T * b + q + 1)
                if q == 0:
                    act.wait_ge(ffn_summed, T * b + 1)
                act.activation(two(prob[:, q % 2, :]), slot(q % 2), ACT.Exp, bias=nmax[:, q:q + 1],
                               accum_out=rsum[:, q:q + 1]).then_inc(exp_set, 1)

            def hi_probs(b, q):
                act.wait_ge(p_turned, T * b + q + 1)
                act.activation(two(pth[:, q % 2, :]), ps[:, PT_BANK:PT_BANK + 2, :], ACT.Copy).then_inc(pth_set, 1)

            def batch(i, s, more):
                b = 2 * i + s
                exponentials(b, 0)
                for q in range(T - 1):
                    hi_probs(b, q)
                    exponentials(b, q + 1)
                if more:
                    hi_rows(b + 1, 0)
                hi_probs(b, T - 1)
                if more:
                    hi_rows(b + 1, 1)
                    hi_queries(b + 1)
                    hi_keys(b + 1)
                for n in range(N2):
                    act.wait_ge(x2_turned, N2 * b + n + 1)
                    act.activation(x2h[:, :, half(n)], slot(n), ACT.Copy).then_inc(x2h_set, 1)
                if more:
                    hi_values(b + 1)
                for j in range(J):
                    act.wait_ge(hidden, J * b + j + 1)
                    if j >= 2:
                        act.wait_ge(gl_set, J * b + j - 1)
                    act.activation(two(g[:, j % 2, :]), slot(1 + j % 2), ACT.Gelu, bias=cols[:, j:j + 1],
                                   scale=alpha1[:, j:j + 1]).then_inc(gelu_set, 1)

            with act.Fori(0, PAIRS - 1) as i:
                batch(i, 0, True)
                batch(i, 1, True)
            batch(PAIRS - 1, 0, True)
            batch(PAIRS - 1, 1, False)

        @block.vector
        def _(dve):
            def stats_attention(b, s, loads, tiles):
                for t in tiles:
                    if t == 0:
                        dve.wait_ge(x_loaded[s], 16 * loads)
                    dve.bn_stats(st1[:, t, :], xin[s][:, t, :]).then_inc(stats1, 1)

            def aggregate_attention(b):
                for t in range(T):
                    dve.bn_aggr(mv1[:, t, :], st1[:, t, :]).then_inc(aggr1, 1)

            def normalize_attention(b, s, tiles):
                for t in tiles:
                    if t == 0:
                        dve.wait_ge(rstd1_set, b + 1)
                    dve.tensor_scalar(xn1[:, t, :], xin[s][:, t, :], mv1[:, t, 0:1], rstd1[:, t:t + 1],
                                      ALU.subtract, ALU.mult).then_inc(xn1_set, 1)

            def lo_rows(b, n):
                dve.wait_ge(xh_set, N2 * b + n + 1)
                dve.tensor_tensor(xl[:, :, half(n)], slot(n), xh[:, :, half(n)].bitcast(F32),
                                  ALU.subtract).then_inc(xl_set, 1)

            def mask_keys(b, n):
                m = mask_bc[:, half(n)].unsqueeze(1).broadcast_to([P, C, HALF])
                dve.scalar_tensor_tensor(out=kmf[:, :, half(n)], in0=slot(n), scalar=1.0, in1=m,
                                         op0=ALU.add, op1=ALU.mult).then_inc(km_set, 1)

            def lo_queries(b):
                for k in range(QG):
                    n, m = divmod(k, C)
                    dve.wait_ge(qh_set, QG * b + k + 1)
                    dve.scalar_tensor_tensor(out=ql[:, m, half(n)], in0=ps[:, PT_BANK + k, :], scalar=ccol[:, m:m + 1],
                                             in1=qh[:, m, half(n)].bitcast(F32), op0=ALU.add,
                                             op1=ALU.subtract).then_inc(ql_set, 1)

            def lo_values(b):
                for k in range(VG):
                    dve.wait_ge(vh_set, VG * b + k + 1)
                    dve.tensor_tensor(vl[:, 2 * k:2 * k + 2, :], two(ps[:, PT_BANK + k, :]),
                                      vh[:, 2 * k:2 * k + 2, :].bitcast(F32), ALU.subtract).then_inc(vl_set, 1)

            def row_max(b, q):
                dve.wait_ge(scored, T * b + q + 1)
                dve.tensor_reduce(nmax[:, q:q + 1], slot(q % 2), mybir.AxisListType.XY, ALU.max,
                                  negate=True).then_inc(max_set, 1)

            def lo_probs(b, q):
                dve.wait_ge(pth_set, T * b + q + 1)
                dve.tensor_tensor(two(ptl[:, q % 2, :]), ps[:, PT_BANK:PT_BANK + 2, :],
                                  two(pth[:, q % 2, :].bitcast(F32)), ALU.subtract).then_inc(ptl_set, 1)

            def invert_sum(q):
                dve.reciprocal(rinv[:, q:q + 1], rsum[:, q:q + 1]).then_inc(rinv_set, 1)

            def add_attention(b, s, q):
                dve.wait_ge(pv_summed, T * b + q + 1)
                dve.wait_ge(rinv_set, T * b + q + 1)
                dve.wait_ge(xbias_added, T * b + q + 1)
                dve.scalar_tensor_tensor(out=xin[s][:, q, :], in0=ps[:, OUT_BANK + q % 2, 0:D], scalar=rinv[:, q:q + 1],
                                         in1=xin[s][:, q, :], op0=ALU.mult, op1=ALU.add).then_inc(x1_set, 1)
                dve.wait_ge(x1_set, T * b + q + 1)
                dve.bn_stats(st2[:, q, :], xin[s][:, q, :]).then_inc(stats2, 1)
                dve.wait_ge(stats2, T * b + q + 1)
                if q < T - 1:
                    invert_sum(q + 1)
                else:
                    normalize_ffn(b, s, q - 1)
                dve.bn_aggr(mv2[:, q, :], st2[:, q, :]).then_inc(aggr2, 1)

            def normalize_ffn(b, s, q):
                dve.wait_ge(rstd2_set, T * b + q + 1)
                dve.tensor_scalar(xn2[:, q, :], xin[s][:, q, :], mv2[:, q, 0:1], rstd2[:, q:q + 1],
                                  ALU.subtract, ALU.mult).then_inc(xn2_set, 1)

            stats_attention(0, 0, 1, range(T))
            dve.wait_ge(stats1, T)
            aggregate_attention(0)
            dve.wait_ge(wqk_loaded, 32)
            dve.tensor_reduce(wkt[:], wk[:], AX_X, ALU.add).then_inc(prep_dve, 1)
            dve.wait_ge(cols_turned, 1)
            dve.tensor_copy(cols[:], ps[:, 7, 0:J + 3 * C]).then_inc(prep_dve, 1)
            dve.wait_ge(prep_dve, 2)
            bq_c, bk_c, bv_c = (cols[:, J + C * n:J + C * (n + 1)] for n in range(3))
            dve.tensor_tensor(wkt[:], bk_c, wkt[:], ALU.subtract).then_inc(prep_dve, 1)
            dve.wait_ge(prep_dve, 3)
            for c in range(C):
                dve.scalar_tensor_tensor(out=wkc[:, c, :], in0=wkt[:, c:c + 1].broadcast_to([P, D]), scalar=1.0 / D,
                                         in1=wk[:, c, :], op0=ALU.mult, op1=ALU.add).then_inc(cols_turned, 1)
            for c in range(C):
                dve.tensor_scalar(bvb[:, c, :], ones[:], bv_c[:, c:c + 1], None, ALU.mult).then_inc(cols_turned, 1)
            normalize_attention(0, 0, range(T))
            dve.wait_ge(prep_pe, 3)
            dve.tensor_copy(woT[:].rearrange("p c d -> p (c d)"), ps[:, 2, :]).then_inc(prep_dve, 1)
            dve.tensor_scalar(ccol[:], ps[:, 1, 0:C], SCALE, None, ALU.mult).then_inc(prep_dve, 1)
            dve.wait_ge(prep_act, 1)
            dve.scalar_tensor_tensor(out=Ml[:].rearrange("p c d -> p (c d)"), in0=ps[:, 0, :], scalar=SCALE,
                                     in1=Mh[:].rearrange("p c d -> p (c d)").bitcast(F32), op0=ALU.mult,
                                     op1=ALU.subtract).then_inc(prep_dve, 1)
            dve.wait_ge(wff_loaded, 32)
            dve.tensor_reduce(alpha1[:], w1s[:], AX_X, ALU.add, apply_absolute_value=True).then_inc(prep_dve, 1)
            dve.tensor_reduce(alpha2[:], w2s[:], AX_X, ALU.add, apply_absolute_value=True).then_inc(prep_dve, 1)
            dve.wait_ge(prep_act, 2)
            dve.tensor_tensor(Nl[:].rearrange("p c d -> p (c d)"), ps[:, 3, :],
                              Nh[:].rearrange("p c d -> p (c d)").bitcast(F32), ALU.subtract).then_inc(prep_dve, 1)
            dve.wait_ge(prep_pe, 5)
            dve.wait_ge(small_loaded, 16 * 7)
            dve.tensor_tensor(bias_bc[:], ps[:, 4, 0:D], bias_bc[:], ALU.add).then_inc(prep_dve, 1)
            dve.wait_ge(prep_dve, 8)
            dve.tensor_scalar(alpha1[:], alpha1[:], 1.0 / D, None, ALU.mult).then_inc(prep_dve, 1)
            for c in range(C):
                dve.tensor_scalar(diag[:, c, :], ident[:], alpha2[:, c:c + 1], 1.0 / H, ALU.mult, ALU.mult).then_inc(prep_dve, 1)
            w2f, negf = w2s[:].rearrange("p c h -> p (c h)"), neg[:].rearrange("p j d -> p (j d)")
            w1f = w1s[:].rearrange("p j d -> p (j d)")
            dve.tensor_scalar(negf, w1f, 0.0, None, ALU.is_lt).then_inc(prep_dve, 1)
            dve.wait_ge(prep_dve, 14)
            dve.scalar_tensor_tensor(out=w1f, in0=w1f, scalar=0.0, in1=negf, op0=ALU.is_gt,
                                     op1=ALU.subtract).then_inc(prep_dve, 1)
            dve.wait_ge(prep_dve, 15)
            dve.tensor_scalar(negf, w2f, 0.0, None, ALU.is_lt).then_inc(prep_dve, 1)
            dve.wait_ge(prep_dve, 16)
            dve.scalar_tensor_tensor(out=w2f, in0=w2f, scalar=0.0, in1=negf, op0=ALU.is_gt,
                                     op1=ALU.subtract).then_inc(prep_dve, 1)
            dve.wait_ge(prep_pe, 6)
            dve.tensor_copy(alpha2_bc[:], ps[:, 4, D:2 * D]).then_inc(prep_dve, 1)
            for k in range(2 * C):
                dve.wait_ge(prep_pe, 7 + k)
                c, n = divmod(k, 2)
                dve.tensor_copy(sgn1[:, c, half(n)], ps[:, 4 + k, :]).then_inc(prep_dve, 1)
            for k in range(J // 2):
                dve.wait_ge(prep_pe, 7 + 2 * C + k)
                dve.tensor_copy(sgn2[:, 2 * k:2 * k + 2, :], two(ps[:, 4 + k, :])).then_inc(prep_dve, 1)

            for n in range(N2):
                lo_rows(0, n)
                mask_keys(0, n)
            lo_queries(0)
            lo_values(0)
            row_max(0, 0)

            def batch(i, s, more):
                b = 2 * i + s
                r, loads = 1 - s, i + 1 + s
                row_max(b, 1)
                lo_probs(b, 0)
                invert_sum(0)
                for q in range(T - 2):
                    if q == 4 and more:
                        dve.wait_ge(stats1, T * (b + 2))
                    row_max(b, q + 2)
                    lo_probs(b, q + 1)
                    if q >= 1:
                        normalize_ffn(b, s, q - 1)
                    if more:
                        if q in (2, 3):
                            stats_attention(b + 1, r, loads, range(TH * (q - 2), TH * (q - 1)))
                        if q == 4:
                            aggregate_attention(b + 1)
                        if q == 5:
                            normalize_attention(b + 1, r, range(T))
                    add_attention(b, s, q)
                if more:
                    lo_rows(b + 1, 0)
                lo_probs(b, T - 1)
                normalize_ffn(b, s, T - 3)
                if more:
                    lo_rows(b + 1, 1)
                add_attention(b, s, T - 2)
                if more:
                    mask_keys(b + 1, 0)
                add_attention(b, s, T - 1)
                if more:
                    mask_keys(b + 1, 1)
                normalize_ffn(b, s, T - 1)
                if more:
                    lo_queries(b + 1)
                for n in range(N2):
                    dve.wait_ge(x2h_set, N2 * b + n + 1)
                    if n == 0:
                        dve.wait_ge(x2_turned, N2 * (b + 1))
                    dve.tensor_tensor(x2l[:, :, half(n)], slot(n), x2h[:, :, half(n)].bitcast(F32),
                                      ALU.subtract).then_inc(x2l_set, 1)
                if more:
                    lo_values(b + 1)
                for j in range(J):
                    dve.wait_ge(gelu_set, J * b + j + 1)
                    if j == 0:
                        dve.wait_ge(kl_set, N2 * (b + 1 + more))
                    dve.tensor_copy(gh[:, j, :], g[:, j % 2, :]).then_inc(gh_set, 1)
                    dve.wait_ge(gh_set, J * b + j + 1)
                    dve.tensor_tensor(gl[:, j, :], g[:, j % 2, :], gh[:, j, :].bitcast(F32),
                                      ALU.subtract).then_inc(gl_set, 1)
                if more:
                    row_max(b + 1, 0)
                for t in range(T):
                    dve.wait_ge(ffn_summed, T * b + t + 2)
                    if t >= 2:
                        dve.wait_ge(y_set, T * b + t - 1)
                    dve.tensor_tensor(ys[:, t % 2, :], ps[:, OUT_BANK + t % 2, 0:D], alpha2_bc[:],
                                      ALU.mult).then_inc(ffn_scaled, 1)

            with dve.Fori(0, PAIRS - 1) as i:
                batch(i, 0, True)
                batch(i, 1, True)
            batch(PAIRS - 1, 0, True)
            batch(PAIRS - 1, 1, False)

        @block.tensor
        def _(pe):
            def turn_rows(b, n):
                pe.wait_ge(xn1_set, T * b + TH * (n + 1))
                for t in range(TH):
                    for c in range(C):
                        last = pe.transpose(ps[:, 2 * n + c, tile(t)], xn1[:, TH * n + t, tile(c)], ident[:])
                last.then_inc(x_turned, 1)

            def queries(b, first):
                for k in range(QG):
                    n, m = divmod(k, C)
                    if m == 0:
                        pe.wait_ge(xl_set, N2 * b + n + 1)
                    if not first and k >= 2:
                        pe.wait_ge(x1_set, T * (b - 1) + T - 3 + k)
                    bank = ps[:, PT_BANK + k, :]
                    for c in range(C):
                        pe.matmul(bank, Mh[:, c, tile(m)], xh[:, c, half(n)], start=c == 0, stop=False)
                        pe.matmul(bank, Mh[:, c, tile(m)], xl[:, c, half(n)], start=False, stop=False)
                    for c in range(C):
                        last = pe.matmul(bank, Ml[:, c, tile(m)], xh[:, c, half(n)], start=False, stop=c == C - 1)
                    last.then_inc(q_summed, 1)

            def values(b):
                for k in range(VG):
                    pe.wait_ge(ql_set, QG * b + k + 1)
                    for t in range(2 * k, 2 * k + 2):
                        bank = ps[:, PT_BANK + k, (t % 2) * D:(t % 2 + 1) * D]
                        for c in range(C):
                            pe.matmul(bank, xh[:, c, tile(t)], Nh[:, c, :], start=c == 0, stop=False)
                            pe.matmul(bank, xh[:, c, tile(t)], Nl[:, c, :], start=False, stop=False)
                        for c in range(C):
                            last = pe.matmul(bank, xl[:, c, tile(t)], Nh[:, c, :], start=False, stop=c == C - 1)
                    last.then_inc(v_summed, 1)

            def scores(b, q):
                if q == 0:
                    pe.wait_ge(kl_set, N2 * (b + 1))
                    pe.wait_ge(ql_set, QG * (b + 1))
                for c in range(C):
                    for part, keys in ((qh, kh), (qh, kl), (ql, kh)):
                        for n in range(N2):
                            last = pe.matmul(ps[:, 2 * (q % 2) + n, :], part[:, c, tile(q)], keys[:, c, half(n)],
                                             start=c == 0 and part is qh and keys is kh,
                                             stop=c == C - 1 and part is ql)
                last.then_inc(scored, 1)

            def turn_probs(b, q):
                pe.wait_ge(exp_set, T * b + q + 1)
                if q >= 1:
                    pe.wait_ge(ptl_set, T * b + q)
                for t in range(T):
                    last = pe.transpose(ps[:, PT_BANK + t // TH, tile(t % TH)], prob[:, q % 2, tile(t)], ident[:])
                last.then_inc(p_turned, 1)

            def weigh_values(b, q):
                if q == 0:
                    pe.wait_ge(vl_set, VG * (b + 1))
                pe.wait_ge(ptl_set, T * b + q + 1)
                if q >= 2:
                    pe.wait_ge(x1_set, T * b + q - 1)
                bank = ps[:, OUT_BANK + q % 2, 0:D]
                for t in range(T):
                    pe.matmul(bank, pth[:, q % 2, tile(t)], vh[:, t, :], start=t == 0, stop=False)
                    pe.matmul(bank, pth[:, q % 2, tile(t)], vl[:, t, :], start=False, stop=False)
                for t in range(T):
                    last = pe.matmul(bank, ptl[:, q % 2, tile(t)], vh[:, t, :], start=False, stop=t == T - 1)
                last.then_inc(pv_summed, 1)

            pe.wait_ge(consts_set, 5)
            pe.wait_ge(small_loaded, 16 * 7)
            pe.transpose(ps[:, 7, 0:J + 3 * C], rows[:], ident[0:J + 3 * C, 0:J + 3 * C]).then_inc(cols_turned, 1)
            pe.wait_ge(wqk_loaded, 32)
            pe.wait_ge(cols_turned, 1 + 2 * C)
            for m in range(C):
                for c in range(C):
                    last = pe.matmul(ps[:, 0, m * D:(m + 1) * D], wq[:, c, tile(m)], wkc[:, c, :],
                                     start=c == 0, stop=c == C - 1)
            last.then_inc(prep_pe, 1)
            for m in range(C):
                for c in range(C):
                    last = pe.matmul(ps[:, 1, m:m + 1], wkc[:, c, tile(m)], cols[:, J + c:J + c + 1],
                                     start=c == 0, stop=c == C - 1)
            last.then_inc(prep_pe, 1)
            pe.wait_ge(wvo_loaded, 32)
            for e in range(C):
                for c in range(C):
                    last = pe.transpose(ps[:, 2, e * D + c * P:e * D + (c + 1) * P], wo[:, c, tile(e)], ident[:])
                if e == 0:
                    last.then_inc(ffn_summed, 1)
            last.then_inc(prep_pe, 1)
            pe.wait_ge(prep_dve, 4)
            for m in range(C):
                for e in range(C):
                    last = pe.matmul(ps[:, 3, m * D:(m + 1) * D], wv[:, e, tile(m)], woT[:, e, :],
                                     start=e == 0, stop=e == C - 1)
            last.then_inc(prep_pe, 1)
            for e in range(C):
                last = pe.matmul(ps[:, 4, 0:D], bvb[:, e, :], woT[:, e, :], start=e == 0, stop=e == C - 1)
            last.then_inc(prep_pe, 1)
            pe.wait_ge(prep_dve, 13)
            for c in range(C):
                last = pe.matmul(ps[:, 4, D + c * P:D + (c + 1) * P], ones[:], diag[:, c, :], start=True, stop=True)
            last.then_inc(prep_pe, 1)
            pe.wait_ge(prep_dve, 18)
            for k in range(2 * C):
                c, n = divmod(k, 2)
                for j in range(4):
                    last = pe.transpose(ps[:, 4 + k, tile(j)], w1s[:, 4 * n + j, tile(c)], ident[:])
                last.then_inc(prep_pe, 1)
            for k in range(J // 2):
                pe.wait_ge(prep_dve, 19 + k)
                for j in range(2):
                    for c in range(C):
                        last = pe.transpose(ps[:, 4 + k, j * D + c * P:j * D + (c + 1) * P],
                                            w2s[:, c, tile(2 * k + j)], ident[:])
                last.then_inc(prep_pe, 1)

            for n in range(N2):
                turn_rows(0, n)
            pe.wait_ge(prep_dve, 18 + 2 * C + J // 2)
            queries(0, True)
            values(0)
            scores(0, 0)

            def batch(i, s, more):
                b = 2 * i + s
                scores(b, 1)
                turn_probs(b, 0)
                for q in range(T - 2):
                    scores(b, q + 2)
                    turn_probs(b, q + 1)
                    weigh_values(b, q)
                if more:
                    turn_rows(b + 1, 0)
                turn_probs(b, T - 1)
                if more:
                    turn_rows(b + 1, 1)
                weigh_values(b, T - 2)
                weigh_values(b, T - 1)
                if more:
                    queries(b + 1, False)
                for n in range(N2):
                    pe.wait_ge(xn2_set, T * b + TH * (n + 1))
                    if more:
                        pe.wait_ge(km_set, N2 * (b + 1) + n + 1)
                    for t in range(TH):
                        for c in range(C):
                            last = pe.transpose(ps[:, 2 * n + c, tile(t)], xn2[:, TH * n + t, tile(c)], ident[:])
                    last.then_inc(x2_turned, 1)
                if more:
                    values(b + 1)
                for j in range(J):
                    if j == 0:
                        pe.wait_ge(x2l_set, N2 * (b + 1))
                    if j == 1 and more:
                        pe.wait_ge(vl_set, VG * (b + 1) + 2)
                    if j >= 2:
                        pe.wait_ge(gelu_set, J * b + j - 1)
                    for c in range(C):
                        for part in (x2h, x2l):
                            for n in range(N2):
                                last = pe.matmul(ps[:, 2 + 2 * (j % 2) + n, :], sgn1[:, c, tile(j)], part[:, c, half(n)],
                                                 start=c == 0 and part is x2h, stop=c == C - 1 and part is x2l)
                    last.then_inc(hidden, 1)
                if more:
                    scores(b + 1, 0)
                for t in range(T):
                    if t < 2 and more:
                        pe.wait_ge(vl_set, VG * (b + 1) + 3 + t)
                    if t >= 2:
                        pe.wait_ge(ffn_scaled, T * b + t - 1)
                    for j in range(J):
                        if t == 0:
                            pe.wait_ge(gl_set, J * b + j + 1)
                        pe.matmul(ps[:, OUT_BANK + t % 2, 0:D], gh[:, j, tile(t)], sgn2[:, j, :], start=j == 0, stop=False)
                        last = pe.matmul(ps[:, OUT_BANK + t % 2, 0:D], gl[:, j, tile(t)], sgn2[:, j, :],
                                         start=False, stop=j == J - 1)
                    last.then_inc(ffn_summed, 1)

            with pe.Fori(0, PAIRS - 1) as i:
                batch(i, 0, True)
                batch(i, 1, True)
            batch(PAIRS - 1, 0, True)
            batch(PAIRS - 1, 1, False)


_INS = ["L0_attn_x", "L0_attn_Wq", "L0_attn_bq", "L0_attn_Wk", "L0_attn_bk", "L0_attn_Wv", "L0_attn_bv",
        "L0_attn_Wo", "L0_attn_bo", "L0_ffn_w1", "L0_ffn_b1", "L0_ffn_w2", "L0_ffn_b2"]


def kernel(**inputs):
    import numpy as _np
    import concourse.bacc as _bacc
    from concourse import mybir as _mybir
    from concourse.bass_utils import run_bass_kernel_spmd as _run

    nc = _bacc.Bacc("TRN2", target_bir_lowering=False, num_devices=1)
    arrays, args = {}, []
    for name in _INS:
        a = _np.ascontiguousarray(inputs[name])
        arrays[f"in_{name}_dram"] = a
        args.append(nc.dram_tensor(f"in_{name}_dram", a.shape, _mybir.dt.from_np(a.dtype), kind="ExternalInput").ap())
    shape = tuple(inputs["L0_attn_x"].shape)
    mask = gaussian_mask_row(shape[1], shape[1] // P)
    arrays["mask_dram"] = mask
    args.append(nc.dram_tensor("mask_dram", mask.shape, _mybir.dt.from_np(mask.dtype), kind="ExternalInput").ap())
    args.append(nc.dram_tensor("out_dram", shape, F32, kind="ExternalOutput").ap())
    preln_attention_ffn(nc, *args)
    r = _run(nc, [arrays], core_ids=[0])
    return r.results[0]["out_dram"]
```

```python
from contextlib import ExitStack

import numpy as np
import concourse.bass as bass
from concourse import mybir

F32 = mybir.dt.float32
F32R = mybir.dt.float32r
ACT = mybir.ActivationFunctionType
ALU = mybir.AluOpType
AX_X = mybir.AxisListType.X

P = 128
HALF = 512
EPS = 1e-5


def gaussian_mask_row(seq, tiles):
    pos = np.arange(seq, dtype=np.float32)
    mask = np.exp(np.float32(-0.5) * ((pos - np.float32(seq / 2)) / np.float32(seq / 4)) ** 2)
    return np.ascontiguousarray(mask.astype(np.float32).reshape(P, tiles).T).reshape(-1)


def preln_attention_ffn(nc, x, Wq, bq, Wk, bk, Wv, bv, Wo, bo, w1, b1, w2, b2, mask, out):
    B, S, D = x.shape
    H = w1.shape[0]
    T = S // P
    C = D // P
    J = H // P
    N2 = S // HALF
    TH = T // N2
    PAIRS = B // 2
    QG = C * N2
    VG = T // 2
    SCALE = float(D) ** -0.5

    x_v = x.rearrange("b (p t) d -> b p t d", t=T)
    out_v = out.rearrange("b (p t) d -> b p t d", t=T)

    with ExitStack() as ctx:
        def sb(name, shape, dt=F32, stack=ctx):
            return stack.enter_context(nc.sbuf_tensor(name, shape, dt))

        def sem(name):
            return ctx.enter_context(nc.semaphore(name))

        ident = sb("ident", [P, P])
        ones = sb("ones", [P, P])
        mask_bc = sb("mask_bc", [P, S])
        bias_bc = sb("bias_bc", [P, D])
        b2_bc = sb("b2_bc", [P, D])
        alpha2_bc = sb("alpha2_bc", [P, D])
        alpha1 = sb("alpha1", [P, J])
        alpha2 = sb("alpha2", [P, C])
        cols = sb("cols", [P, J + 3 * C])
        ccol = sb("ccol", [P, C])
        wkt = sb("wkt", [P, C])
        Mh = sb("Mh", [P, C, D], F32R)
        Ml = sb("Ml", [P, C, D], F32R)
        Nh = sb("Nh", [P, C, D], F32R)
        Nl = sb("Nl", [P, C, D], F32R)
        sgn1 = sb("sgn1", [P, C, H], F32R)
        sgn2 = sb("sgn2", [P, J, D], F32R)
        xin = [sb(f"xin{s}", [P, T, D]) for s in range(2)]
        kh = sb("kh", [P, C, S], F32R)
        kl = sb("kl", [P, C, S], F32R)
        qh = sb("qh", [P, C, S], F32R)
        ql = sb("ql", [P, C, S], F32R)
        vhl = sb("vhl", [P, T, 2, D], F32R)
        vh, vl = vhl[:, :, 0, :], vhl[:, :, 1, :]
        g = sb("g", [P, 2, S])
        ys = sb("ys", [P, 2, D])
        mhalf = sb("mhalf", [P, T])
        eps = sb("eps", [P, T])
        st1 = sb("st1", [P, T, 6])
        mv1 = sb("mv1", [P, T, 2])
        ve1 = sb("ve1", [P, T])
        rstd1 = sb("rstd1", [P, T])
        st2 = sb("st2", [P, T, 6])
        mv2 = sb("mv2", [P, T, 2])
        ve2 = sb("ve2", [P, T])
        rstd2 = sb("rstd2", [P, T])
        nmax = sb("nmax", [P, T])
        rsum = sb("rsum", [P, T])
        rinv = sb("rinv", [P, T])

        with ExitStack() as place:
            xn1 = sb("xn1", [P, T, D], F32, place)
            xn2 = sb("xn2", [P, T, D], F32, place)
        with ExitStack() as place:
            x2h = sb("x2h", [P, C, S], F32R, place)
            x2l = sb("x2l", [P, C, S], F32R, place)
            with ExitStack() as inner:
                xh = sb("xh", [P, C, S], F32R, inner)
                xl = sb("xl", [P, C, S], F32R, inner)
                kmf = sb("kmf", [P, C, S], F32, inner)
                prob = sb("prob", [P, 2, S], F32, inner)
                pth = sb("pth", [P, 2, S], F32R, inner)
                ptl = sb("ptl", [P, 2, S], F32R, inner)
            with ExitStack() as inner:
                sb("gap", [P, 3 * C * S], F32, inner)
                wq = sb("wq", [P, C, D], F32, inner)
                wk = sb("wk", [P, C, D], F32, inner)
                wv = sb("wv", [P, C, D], F32, inner)
                wo = sb("wo", [P, C, D], F32, inner)
                wkc = sb("wkc", [P, C, D], F32, inner)
                woT = sb("woT", [P, C, D], F32, inner)
                w1s = sb("w1s", [P, J, D], F32, inner)
                w2s = sb("w2s", [P, C, H], F32, inner)
                neg = sb("neg", [P, J, D], F32, inner)
                rows = sb("rows", [J + 3 * C, P], F32, inner)
                bvb = sb("bvb", [P, C, P], F32, inner)
                diag = sb("diag", [P, C, P], F32, inner)
            gh = sb("gh", [P, J, S], F32R, place)
            gl = sb("gl", [P, J, S], F32R, place)

        ps = ctx.enter_context(nc.psum_tensor("ps", [P, 8, HALF], F32))
        PT_BANK, OUT_BANK = 4, 6

        x_loaded = [sem(f"x_loaded{s}") for s in range(2)]
        wqk_loaded, wvo_loaded, w1_loaded, w2_loaded, rows_loaded, bcast_loaded = (
            sem(n) for n in ("wqk_loaded", "wvo_loaded", "w1_loaded", "w2_loaded", "rows_loaded", "bcast_loaded"))
        consts_set, rows_turned, cols_set, wkc_set, m_summed, mh_set, ml_set, c_summed, ccol_set = (
            sem(n) for n in ("consts_set", "rows_turned", "cols_set", "wkc_set", "m_summed", "mh_set", "ml_set",
                             "c_summed", "ccol_set"))
        wo_turned, woT_set, bvb_set, n_summed, nh_set, nl_set, bias_summed, bias_set = (
            sem(n) for n in ("wo_turned", "woT_set", "bvb_set", "n_summed", "nh_set", "nl_set", "bias_summed",
                             "bias_set"))
        alphas_set, diag_set, alpha2_spread, alpha2_set, neg_set, signs_set, signs_turned, sgn1_set, sgn2_set = (
            sem(n) for n in ("alphas_set", "diag_set", "alpha2_spread", "alpha2_set", "neg_set", "signs_set",
                             "signs_turned", "sgn1_set", "sgn2_set"))
        y_stored = sem("y_stored")
        stats1, aggr1, vareps1, rstd1_set, xn1_set, xbias_added = (
            sem(n) for n in ("stats1", "aggr1", "vareps1", "rstd1_set", "xn1_set", "xbias_added"))
        x_turned, xh_set, xl_set, km_set, kh_set, kl_set = (
            sem(n) for n in ("x_turned", "xh_set", "xl_set", "km_set", "kh_set", "kl_set"))
        q_summed, qh_set, ql_set, v_summed, vh_set, vl_set = (
            sem(n) for n in ("q_summed", "qh_set", "ql_set", "v_summed", "vh_set", "vl_set"))
        scored, max_set, exp_set, p_turned, pth_set, ptl_set, rinv_set, pv_summed, x1_half, x1_set = (
            sem(n) for n in ("scored", "max_set", "exp_set", "p_turned", "pth_set", "ptl_set", "rinv_set",
                             "pv_summed", "x1_half", "x1_set"))
        stats2, aggr2, vareps2, rstd2_set, xn2_set, b2_added = (
            sem(n) for n in ("stats2", "aggr2", "vareps2", "rstd2_set", "xn2_set", "b2_added"))
        x2_turned, x2h_set, x2l_set, hidden, gelu_set, gh_set, gl_set = (
            sem(n) for n in ("x2_turned", "x2h_set", "x2l_set", "hidden", "gelu_set", "gh_set", "gl_set"))
        ffn_summed, ffn_scaled, y_set = (sem(n) for n in ("ffn_summed", "ffn_scaled", "y_set"))

        block = ctx.enter_context(nc.Block())

        def slot(s):
            return ps[:, 2 * s:2 * s + 2, :]

        def two(ap):
            return ap.rearrange("p (a n) -> p a n", a=2)

        def half(n):
            return slice(n * HALF, (n + 1) * HALF)

        def tile(t):
            return slice(t * P, (t + 1) * P)


        @block.sync
        def _(sp):
            sp.dma_start(xin[0][:], x_v[0]).then_inc(x_loaded[0], 16)
            sp.dma_start(wk[:], Wk.rearrange("(c p) d -> p c d", p=P)).then_inc(wqk_loaded, 16)
            sp.dma_start(wq[:], Wq.rearrange("(c p) d -> p c d", p=P)).then_inc(wqk_loaded, 16)
            sp.dma_start(wo[:], Wo.rearrange("(c p) d -> p c d", p=P)).then_inc(wvo_loaded, 16)
            sp.dma_start(wv[:], Wv.rearrange("(c p) d -> p c d", p=P)).then_inc(wvo_loaded, 16)
            sp.dma_start(w1s[:], w1.rearrange("(j p) d -> p j d", p=P)).then_inc(w1_loaded, 16)
            sp.dma_start(w2s[:], w2.rearrange("(c p) h -> p c h", p=P)).then_inc(w2_loaded, 16)
            sp.dma_start(xin[1][:], x_v[1]).then_inc(x_loaded[1], 16)

            def store_and_load(i, s, more):
                b = 2 * i + s
                for n in range(N2):
                    sp.wait_ge(y_set, T * b + TH * (n + 1))
                    sp.dma_start(out_v[b, :, n * TH:(n + 1) * TH, :],
                                 xin[s][:, n * TH:(n + 1) * TH, :]).then_inc(y_stored, 16)
                if more:
                    sp.wait_ge(y_stored, 16 * N2 * (b + 1))
                    sp.dma_start(xin[s][:], x_v[b + 2]).then_inc(x_loaded[s], 16)

            with sp.Fori(0, PAIRS - 1) as i:
                store_and_load(i, 0, True)
                store_and_load(i, 1, True)
            store_and_load(PAIRS - 1, 0, False)
            store_and_load(PAIRS - 1, 1, False)
            sp.wait_ge(y_stored, 16 * N2 * B)

        @block.gpsimd
        def _(pool):
            pool.memset(ident[:], 0.0).then_inc(consts_set, 1)
            pool.memset(ones[:], 1.0).then_inc(consts_set, 1)
            pool.memset(mhalf[:], -0.5).then_inc(consts_set, 1)
            pool.memset(eps[:], EPS).then_inc(consts_set, 1)
            pool.wait_ge(consts_set, 4)
            pool.affine_select(out=ident[:], in_=ident[:], compare_op=ALU.not_equal, fill=1.0, base=0,
                               pattern=[[-1, P]], channel_multiplier=1).then_inc(consts_set, 1)

            def rstd_attention(b):
                pool.wait_ge(aggr1, T * (b + 1))
                pool.tensor_tensor(ve1[:], mv1[:, :, 1], eps[:], ALU.add).then_inc(vareps1, 1)
                pool.wait_ge(vareps1, b + 1)
                pool.tensor_tensor(rstd1[:], ve1[:], mhalf[:], ALU.pow).then_inc(rstd1_set, 1)

            def rstd_ffn(b, q):
                pool.wait_ge(aggr2, T * b + q + 1)
                pool.tensor_tensor(ve2[:, q:q + 1], mv2[:, q, 1:2], eps[:, q:q + 1], ALU.add).then_inc(vareps2, 1)
                pool.wait_ge(vareps2, T * b + q + 1)
                pool.tensor_tensor(rstd2[:, q:q + 1], ve2[:, q:q + 1], mhalf[:, q:q + 1],
                                   ALU.pow).then_inc(rstd2_set, 1)

            def split_keys(b):
                for n in range(N2):
                    pool.wait_ge(kh_set, N2 * b + n + 1)
                    pool.tensor_tensor(kl[:, :, half(n)], kmf[:, :, half(n)],
                                       kh[:, :, half(n)].bitcast(F32), ALU.subtract).then_inc(kl_set, 1)

            def add_bias(b, s, t):
                if t == 0:
                    pool.wait_ge(xn1_set, T * (b + 1))
                pool.tensor_tensor(xin[s][:, t, :], xin[s][:, t, :], bias_bc[:], ALU.add).then_inc(xbias_added, 1)

            rstd_attention(0)
            split_keys(0)
            pool.wait_ge(bias_set, 1)
            for t in range(T):
                add_bias(0, 0, t)

            def batch(i, s, more):
                b = 2 * i + s
                for q in range(TH):
                    rstd_ffn(b, q)
                if more:
                    rstd_attention(b + 1)
                for q in range(TH, T):
                    rstd_ffn(b, q)
                if more:
                    split_keys(b + 1)
                for j in range(J):
                    if j == 0:
                        pool.wait_ge(xn2_set, T * (b + 1))
                    pool.tensor_tensor(xin[s][:, j, :], xin[s][:, j, :], b2_bc[:], ALU.add).then_inc(b2_added, 1)
                for t in range(T):
                    if t == 0:
                        pool.wait_ge(b2_added, T * (b + 1))
                    pool.wait_ge(ffn_scaled, T * b + t + 1)
                    pool.tensor_tensor(xin[s][:, t, :], xin[s][:, t, :], ys[:, t % 2, :], ALU.add).then_inc(y_set, 1)
                    if more:
                        add_bias(b + 1, 1 - s, t)

            with pool.Fori(0, PAIRS - 1) as i:
                batch(i, 0, True)
                batch(i, 1, True)
            batch(PAIRS - 1, 0, True)
            batch(PAIRS - 1, 1, False)

        @block.scalar
        def _(act):
            act.dma_start(rows[0:J, :], b1.rearrange("(j p) -> j p", p=P)).then_inc(rows_loaded, 16)
            for n, b_dram in enumerate((bq, bk, bv)):
                act.dma_start(rows[J + C * n:J + C * (n + 1), :],
                              b_dram.rearrange("(c p) -> c p", p=P)).then_inc(rows_loaded, 16)
            act.dma_start(bias_bc[:], bo.partition_broadcast(P)).then_inc(bcast_loaded, 16)
            act.dma_start(mask_bc[:], mask.partition_broadcast(P)).then_inc(bcast_loaded, 16)
            act.dma_start(b2_bc[:], b2.partition_broadcast(P)).then_inc(bcast_loaded, 16)

            def hi_rows(b, n):
                act.wait_ge(x_turned, N2 * b + n + 1)
                act.activation(xh[:, :, half(n)], slot(n), ACT.Copy).then_inc(xh_set, 1)

            def hi_queries(b):
                for k in range(QG):
                    n, m = divmod(k, C)
                    act.wait_ge(q_summed, QG * b + k + 1)
                    act.activation(qh[:, m, half(n)], ps[:, PT_BANK + k, :], ACT.Identity,
                                   bias=ccol[:, m:m + 1]).then_inc(qh_set, 1)

            def hi_values(b):
                for k in range(VG):
                    act.wait_ge(v_summed, VG * b + k + 1)
                    act.activation(vh[:, 2 * k:2 * k + 2], two(ps[:, PT_BANK + k, :]), ACT.Copy).then_inc(vh_set, 1)

            def hi_keys(b):
                for n in range(N2):
                    act.wait_ge(km_set, N2 * b + n + 1)
                    act.activation(kh[:, :, half(n)], kmf[:, :, half(n)], ACT.Copy).then_inc(kh_set, 1)

            act.wait_ge(wo_turned, 1)
            act.activation(woT[:].rearrange("p c d -> p (c d)"), ps[:, 2, :], ACT.Copy).then_inc(woT_set, 1)
            act.wait_ge(m_summed, 1)
            act.activation(Mh[:].rearrange("p c d -> p (c d)"), ps[:, 4, :], ACT.Copy, scale=SCALE).then_inc(mh_set, 1)
            for n in range(N2):
                hi_rows(0, n)
            act.wait_ge(n_summed, 1)
            act.activation(Nh[:].rearrange("p c d -> p (c d)"), ps[:, 7, :], ACT.Copy).then_inc(nh_set, 1)
            act.wait_ge(ccol_set, 1)
            hi_queries(0)
            hi_keys(0)
            hi_values(0)
            for k in range(J // 2):
                act.wait_ge(signs_turned, 2 * C + k + 1)
                act.activation(sgn2[:, 2 * k:2 * k + 2, :], two(ps[:, 4 + k, :]), ACT.Copy).then_inc(sgn2_set, 1)

            def exponentials(b, q):
                act.wait_ge(max_set, T * b + q + 1)
                if q == 0:
                    act.wait_ge(ffn_summed, T * b + 1)
                act.activation(two(prob[:, q % 2, :]), slot(q % 2), ACT.Exp, bias=nmax[:, q:q + 1],
                               accum_out=rsum[:, q:q + 1]).then_inc(exp_set, 1)

            def hi_probs(b, q):
                act.wait_ge(p_turned, T * b + q + 1)
                act.activation(two(pth[:, q % 2, :]), ps[:, PT_BANK:PT_BANK + 2, :], ACT.Copy).then_inc(pth_set, 1)

            def batch(i, s, more):
                b = 2 * i + s
                exponentials(b, 0)
                for q in range(T - 1):
                    hi_probs(b, q)
                    exponentials(b, q + 1)
                if more:
                    hi_rows(b + 1, 0)
                hi_probs(b, T - 1)
                if more:
                    hi_rows(b + 1, 1)
                    hi_queries(b + 1)
                    hi_keys(b + 1)
                for n in range(N2):
                    act.wait_ge(x2_turned, N2 * b + n + 1)
                    act.activation(x2h[:, :, half(n)], slot(n), ACT.Copy).then_inc(x2h_set, 1)
                if more:
                    hi_values(b + 1)
                for j in range(J):
                    act.wait_ge(hidden, J * b + j + 1)
                    if j >= 2:
                        act.wait_ge(gl_set, J * b + j - 1)
                    act.activation(two(g[:, j % 2, :]), slot(1 + j % 2), ACT.Gelu, bias=cols[:, j:j + 1],
                                   scale=alpha1[:, j:j + 1]).then_inc(gelu_set, 1)

            with act.Fori(0, PAIRS - 1) as i:
                batch(i, 0, True)
                batch(i, 1, True)
            batch(PAIRS - 1, 0, True)
            batch(PAIRS - 1, 1, False)

        @block.vector
        def _(dve):
            def stats_attention(b, s, loads, tiles):
                for t in tiles:
                    if t == 0:
                        dve.wait_ge(x_loaded[s], 16 * loads)
                    dve.bn_stats(st1[:, t, :], xin[s][:, t, :]).then_inc(stats1, 1)

            def aggregate_attention(b):
                for t in range(T):
                    dve.bn_aggr(mv1[:, t, :], st1[:, t, :]).then_inc(aggr1, 1)

            def normalize_attention(b, s, tiles):
                for t in tiles:
                    if t == 0:
                        dve.wait_ge(rstd1_set, b + 1)
                    dve.tensor_scalar(xn1[:, t, :], xin[s][:, t, :], mv1[:, t, 0:1], rstd1[:, t:t + 1],
                                      ALU.subtract, ALU.mult).then_inc(xn1_set, 1)

            def lo_rows(b, n):
                dve.wait_ge(xh_set, N2 * b + n + 1)
                dve.tensor_tensor(xl[:, :, half(n)], slot(n), xh[:, :, half(n)].bitcast(F32),
                                  ALU.subtract).then_inc(xl_set, 1)

            def mask_keys(b, n):
                m = mask_bc[:, half(n)].unsqueeze(1).broadcast_to([P, C, HALF])
                dve.scalar_tensor_tensor(out=kmf[:, :, half(n)], in0=slot(n), scalar=1.0, in1=m,
                                         op0=ALU.add, op1=ALU.mult).then_inc(km_set, 1)

            def lo_queries(b):
                for k in range(QG):
                    n, m = divmod(k, C)
                    dve.wait_ge(qh_set, QG * b + k + 1)
                    dve.scalar_tensor_tensor(out=ql[:, m, half(n)], in0=ps[:, PT_BANK + k, :], scalar=ccol[:, m:m + 1],
                                             in1=qh[:, m, half(n)].bitcast(F32), op0=ALU.add,
                                             op1=ALU.subtract).then_inc(ql_set, 1)

            def lo_values(b):
                for k in range(VG):
                    dve.wait_ge(vh_set, VG * b + k + 1)
                    dve.tensor_tensor(vl[:, 2 * k:2 * k + 2], two(ps[:, PT_BANK + k, :]),
                                      vh[:, 2 * k:2 * k + 2].bitcast(F32), ALU.subtract).then_inc(vl_set, 1)

            def row_max(b, q):
                dve.wait_ge(scored, T * b + q + 1)
                dve.tensor_reduce(nmax[:, q:q + 1], slot(q % 2), mybir.AxisListType.XY, ALU.max,
                                  negate=True).then_inc(max_set, 1)

            def lo_probs(b, q):
                dve.wait_ge(pth_set, T * b + q + 1)
                dve.tensor_tensor(two(ptl[:, q % 2, :]), ps[:, PT_BANK:PT_BANK + 2, :],
                                  two(pth[:, q % 2, :].bitcast(F32)), ALU.subtract).then_inc(ptl_set, 1)

            def invert_sum(q):
                dve.reciprocal(rinv[:, q:q + 1], rsum[:, q:q + 1]).then_inc(rinv_set, 1)

            def add_attention(b, s, q):
                dve.wait_ge(pv_summed, T * b + q + 1)
                dve.wait_ge(rinv_set, T * b + q + 1)
                dve.wait_ge(xbias_added, T * b + q + 1)
                dve.scalar_tensor_tensor(out=xin[s][:, q, :], in0=ps[:, OUT_BANK + q % 2, D:2 * D], scalar=rinv[:, q:q + 1],
                                         in1=xin[s][:, q, :], op0=ALU.mult, op1=ALU.add).then_inc(x1_half, 1)
                dve.wait_ge(x1_half, T * b + q + 1)
                dve.scalar_tensor_tensor(out=xin[s][:, q, :], in0=ps[:, OUT_BANK + q % 2, 0:D], scalar=rinv[:, q:q + 1],
                                         in1=xin[s][:, q, :], op0=ALU.mult, op1=ALU.add).then_inc(x1_set, 1)
                dve.wait_ge(x1_set, T * b + q + 1)
                dve.bn_stats(st2[:, q, :], xin[s][:, q, :]).then_inc(stats2, 1)
                dve.wait_ge(stats2, T * b + q + 1)
                if q < T - 1:
                    invert_sum(q + 1)
                else:
                    normalize_ffn(b, s, q - 1)
                dve.bn_aggr(mv2[:, q, :], st2[:, q, :]).then_inc(aggr2, 1)

            def normalize_ffn(b, s, q):
                dve.wait_ge(rstd2_set, T * b + q + 1)
                dve.tensor_scalar(xn2[:, q, :], xin[s][:, q, :], mv2[:, q, 0:1], rstd2[:, q:q + 1],
                                  ALU.subtract, ALU.mult).then_inc(xn2_set, 1)

            stats_attention(0, 0, 1, range(T))
            dve.wait_ge(stats1, T)
            aggregate_attention(0)
            dve.wait_ge(rows_turned, 1)
            dve.tensor_copy(cols[:], ps[:, 3, 0:J + 3 * C]).then_inc(cols_set, 1)
            dve.wait_ge(wqk_loaded, 32)
            dve.tensor_reduce(wkt[:], wk[:], AX_X, ALU.add).then_inc(wkc_set, 1)
            dve.wait_ge(cols_set, 1)
            dve.wait_ge(wkc_set, 1)
            bk_c, bv_c = (cols[:, J + C * n:J + C * (n + 1)] for n in (1, 2))
            dve.tensor_tensor(wkt[:], bk_c, wkt[:], ALU.subtract).then_inc(wkc_set, 1)
            dve.wait_ge(wkc_set, 2)
            for c in range(C):
                dve.scalar_tensor_tensor(out=wkc[:, c, :], in0=wkt[:, c:c + 1].broadcast_to([P, D]), scalar=1.0 / D,
                                         in1=wk[:, c, :], op0=ALU.mult, op1=ALU.add).then_inc(wkc_set, 1)
            for c in range(C):
                dve.tensor_scalar(bvb[:, c, :], ones[:], bv_c[:, c:c + 1], None, ALU.mult).then_inc(bvb_set, 1)
            normalize_attention(0, 0, range(T))
            w1f, w2f = w1s[:].rearrange("p j d -> p (j d)"), w2s[:].rearrange("p c h -> p (c h)")
            negf = neg[:].rearrange("p j d -> p (j d)")
            dve.wait_ge(w1_loaded, 16)
            dve.tensor_reduce(alpha1[:], w1s[:], AX_X, ALU.add, apply_absolute_value=True).then_inc(alphas_set, 1)
            dve.wait_ge(mh_set, 1)
            dve.scalar_tensor_tensor(out=Ml[:].rearrange("p c d -> p (c d)"), in0=ps[:, 4, :], scalar=SCALE,
                                     in1=Mh[:].rearrange("p c d -> p (c d)").bitcast(F32), op0=ALU.mult,
                                     op1=ALU.subtract).then_inc(ml_set, 1)
            dve.tensor_scalar(negf, w1f, 0.0, None, ALU.is_lt).then_inc(neg_set, 1)
            dve.wait_ge(neg_set, 1)
            dve.scalar_tensor_tensor(out=w1f, in0=w1f, scalar=0.0, in1=negf, op0=ALU.is_gt,
                                     op1=ALU.subtract).then_inc(signs_set, 1)
            for n in range(N2):
                lo_rows(0, n)
            dve.wait_ge(nh_set, 1)
            dve.tensor_tensor(Nl[:].rearrange("p c d -> p (c d)"), ps[:, 7, :],
                              Nh[:].rearrange("p c d -> p (c d)").bitcast(F32), ALU.subtract).then_inc(nl_set, 1)
            dve.wait_ge(bias_summed, 1)
            dve.wait_ge(bcast_loaded, 16 * 3)
            dve.tensor_tensor(bias_bc[:], ps[:, 6, 0:D], bias_bc[:], ALU.add).then_inc(bias_set, 1)
            dve.wait_ge(c_summed, 1)
            dve.tensor_scalar(ccol[:], ps[:, 5, 0:C], SCALE, None, ALU.mult).then_inc(ccol_set, 1)
            for n in range(N2):
                mask_keys(0, n)
            dve.wait_ge(w2_loaded, 16)
            dve.tensor_reduce(alpha2[:], w2s[:], AX_X, ALU.add, apply_absolute_value=True).then_inc(alphas_set, 1)
            lo_queries(0)
            dve.wait_ge(signs_set, 1)
            dve.tensor_scalar(negf, w2f, 0.0, None, ALU.is_lt).then_inc(neg_set, 1)
            dve.wait_ge(neg_set, 2)
            dve.scalar_tensor_tensor(out=w2f, in0=w2f, scalar=0.0, in1=negf, op0=ALU.is_gt,
                                     op1=ALU.subtract).then_inc(signs_set, 1)
            lo_values(0)
            dve.wait_ge(alphas_set, 2)
            for c in range(C):
                dve.tensor_scalar(diag[:, c, :], ident[:], alpha2[:, c:c + 1], 1.0 / H, ALU.mult,
                                  ALU.mult).then_inc(diag_set, 1)
            dve.tensor_scalar(alpha1[:], alpha1[:], 1.0 / D, None, ALU.mult).then_inc(alphas_set, 1)
            for k in range(2 * C):
                c, n = divmod(k, 2)
                dve.wait_ge(signs_turned, k + 1)
                dve.tensor_copy(sgn1[:, c, half(n)], ps[:, k, :]).then_inc(sgn1_set, 1)
            dve.wait_ge(alpha2_spread, 1)
            dve.tensor_copy(alpha2_bc[:], ps[:, 2, 0:D]).then_inc(alpha2_set, 1)
            row_max(0, 0)

            def batch(i, s, more):
                b = 2 * i + s
                r, loads = 1 - s, i + 1 + s
                row_max(b, 1)
                lo_probs(b, 0)
                invert_sum(0)
                for q in range(T - 2):
                    if q == 4 and more:
                        dve.wait_ge(stats1, T * (b + 2))
                    if q == 5 and more:
                        normalize_attention(b + 1, r, range(TH))
                    row_max(b, q + 2)
                    lo_probs(b, q + 1)
                    if q >= 1:
                        normalize_ffn(b, s, q - 1)
                    if more:
                        if q in (2, 3):
                            stats_attention(b + 1, r, loads, range(TH * (q - 2), TH * (q - 1)))
                        if q == 4:
                            aggregate_attention(b + 1)
                        if q == 5:
                            normalize_attention(b + 1, r, range(TH, T))
                    add_attention(b, s, q)
                lo_probs(b, T - 1)
                if more:
                    lo_rows(b + 1, 0)
                normalize_ffn(b, s, T - 3)
                if more:
                    lo_rows(b + 1, 1)
                add_attention(b, s, T - 2)
                if more:
                    mask_keys(b + 1, 0)
                add_attention(b, s, T - 1)
                if more:
                    mask_keys(b + 1, 1)
                normalize_ffn(b, s, T - 1)
                if more:
                    lo_queries(b + 1)
                for n in range(N2):
                    dve.wait_ge(x2h_set, N2 * b + n + 1)
                    if n == 0:
                        dve.wait_ge(x2_turned, N2 * (b + 1))
                    dve.tensor_tensor(x2l[:, :, half(n)], slot(n), x2h[:, :, half(n)].bitcast(F32),
                                      ALU.subtract).then_inc(x2l_set, 1)
                if more:
                    lo_values(b + 1)
                for j in range(J):
                    dve.wait_ge(gelu_set, J * b + j + 1)
                    if j == 0:
                        dve.wait_ge(kl_set, N2 * (b + 1 + more))
                    dve.tensor_copy(gh[:, j, :], g[:, j % 2, :]).then_inc(gh_set, 1)
                    dve.wait_ge(gh_set, J * b + j + 1)
                    dve.tensor_tensor(gl[:, j, :], g[:, j % 2, :], gh[:, j, :].bitcast(F32),
                                      ALU.subtract).then_inc(gl_set, 1)
                if more:
                    row_max(b + 1, 0)
                for t in range(T):
                    dve.wait_ge(ffn_summed, T * b + t + 2)
                    if t >= 2:
                        dve.wait_ge(y_set, T * b + t - 1)
                    dve.tensor_tensor(ys[:, t % 2, :], ps[:, OUT_BANK + t % 2, 0:D], alpha2_bc[:],
                                      ALU.mult).then_inc(ffn_scaled, 1)

            with dve.Fori(0, PAIRS - 1) as i:
                batch(i, 0, True)
                batch(i, 1, True)
            batch(PAIRS - 1, 0, True)
            batch(PAIRS - 1, 1, False)

        @block.tensor
        def _(pe):
            def turn_rows(b, n):
                pe.wait_ge(xn1_set, T * b + TH * (n + 1))
                for t in range(TH):
                    for c in range(C):
                        last = pe.transpose(ps[:, 2 * n + c, tile(t)], xn1[:, TH * n + t, tile(c)], ident[:])
                last.then_inc(x_turned, 1)

            def queries(b, first):
                for k in range(QG):
                    n, m = divmod(k, C)
                    if m == 0:
                        pe.wait_ge(xl_set, N2 * b + n + 1)
                    if not first and k >= 2:
                        pe.wait_ge(x1_set, T * (b - 1) + T - 3 + k)
                    bank = ps[:, PT_BANK + k, :]
                    for c in range(C):
                        pe.matmul(bank, Mh[:, c, tile(m)], xh[:, c, half(n)], start=c == 0, stop=False)
                        pe.matmul(bank, Mh[:, c, tile(m)], xl[:, c, half(n)], start=False, stop=False)
                    for c in range(C):
                        last = pe.matmul(bank, Ml[:, c, tile(m)], xh[:, c, half(n)], start=False, stop=c == C - 1)
                    last.then_inc(q_summed, 1)

            def values(b):
                for k in range(VG):
                    pe.wait_ge(ql_set, QG * b + k + 1)
                    for t in range(2 * k, 2 * k + 2):
                        bank = ps[:, PT_BANK + k, (t % 2) * D:(t % 2 + 1) * D]
                        for c in range(C):
                            pe.matmul(bank, xh[:, c, tile(t)], Nh[:, c, :], start=c == 0, stop=False)
                            pe.matmul(bank, xh[:, c, tile(t)], Nl[:, c, :], start=False, stop=False)
                        for c in range(C):
                            last = pe.matmul(bank, xl[:, c, tile(t)], Nh[:, c, :], start=False, stop=c == C - 1)
                    last.then_inc(v_summed, 1)

            def scores(b, q):
                if q == 0:
                    pe.wait_ge(kl_set, N2 * (b + 1))
                    pe.wait_ge(ql_set, QG * (b + 1))
                for c in range(C):
                    for part, keys in ((qh, kh), (qh, kl), (ql, kh)):
                        for n in range(N2):
                            last = pe.matmul(ps[:, 2 * (q % 2) + n, :], part[:, c, tile(q)], keys[:, c, half(n)],
                                             start=c == 0 and part is qh and keys is kh,
                                             stop=c == C - 1 and part is ql)
                last.then_inc(scored, 1)

            def turn_probs(b, q):
                pe.wait_ge(exp_set, T * b + q + 1)
                if q >= 1:
                    pe.wait_ge(ptl_set, T * b + q)
                for t in range(T):
                    last = pe.transpose(ps[:, PT_BANK + t // TH, tile(t % TH)], prob[:, q % 2, tile(t)], ident[:])
                last.then_inc(p_turned, 1)

            def weigh_values(b, q):
                if q == 0:
                    pe.wait_ge(vl_set, VG * (b + 1))
                pe.wait_ge(ptl_set, T * b + q + 1)
                if q >= 2:
                    pe.wait_ge(x1_set, T * b + q - 1)
                bank = ps[:, OUT_BANK + q % 2, :]
                for t in range(T):
                    pe.matmul(bank, pth[:, q % 2, tile(t)], vhl[:, t, :, :], start=t == 0, stop=False)
                for t in range(T):
                    last = pe.matmul(bank[:, 0:D], ptl[:, q % 2, tile(t)], vh[:, t, :], start=False, stop=t == T - 1)
                last.then_inc(pv_summed, 1)

            pe.wait_ge(consts_set, 5)
            pe.wait_ge(rows_loaded, 16 * 4)
            pe.transpose(ps[:, 3, 0:J + 3 * C], rows[:], ident[0:J + 3 * C, 0:J + 3 * C]).then_inc(rows_turned, 1)
            pe.wait_ge(wvo_loaded, 32)
            for e in range(C):
                for c in range(C):
                    last = pe.transpose(ps[:, 2, e * D + c * P:e * D + (c + 1) * P], wo[:, c, tile(e)], ident[:])
                if e == 0:
                    last.then_inc(ffn_summed, 1)
            last.then_inc(wo_turned, 1)
            pe.wait_ge(wqk_loaded, 32)
            pe.wait_ge(wkc_set, 2 + C)
            for m in range(C):
                for c in range(C):
                    last = pe.matmul(ps[:, 4, m * D:(m + 1) * D], wq[:, c, tile(m)], wkc[:, c, :],
                                     start=c == 0, stop=c == C - 1)
            last.then_inc(m_summed, 1)
            pe.wait_ge(woT_set, 1)
            pe.wait_ge(bvb_set, C)
            for n in range(N2):
                turn_rows(0, n)
            for m in range(C):
                for e in range(C):
                    last = pe.matmul(ps[:, 7, m * D:(m + 1) * D], wv[:, e, tile(m)], woT[:, e, :],
                                     start=e == 0, stop=e == C - 1)
            last.then_inc(n_summed, 1)
            for e in range(C):
                last = pe.matmul(ps[:, 6, 0:D], bvb[:, e, :], woT[:, e, :], start=e == 0, stop=e == C - 1)
            last.then_inc(bias_summed, 1)
            for m in range(C):
                for c in range(C):
                    last = pe.matmul(ps[:, 5, m:m + 1], wkc[:, c, tile(m)], cols[:, J + c:J + c + 1],
                                     start=c == 0, stop=c == C - 1)
            last.then_inc(c_summed, 1)

            pe.wait_ge(ml_set, 1)
            pe.wait_ge(ccol_set, 1)
            pe.wait_ge(bias_set, 1)
            queries(0, True)
            values(0)
            for k in range(2 * C):
                if k == 0:
                    pe.wait_ge(km_set, N2)
                    pe.wait_ge(signs_set, 1)
                c, n = divmod(k, 2)
                for j in range(4):
                    last = pe.transpose(ps[:, k, tile(j)], w1s[:, 4 * n + j, tile(c)], ident[:])
                last.then_inc(signs_turned, 1)
            for k in range(J // 2):
                pe.wait_ge(vl_set, k + 1)
                if k == 0:
                    pe.wait_ge(signs_set, 2)
                for j in range(2):
                    for c in range(C):
                        last = pe.transpose(ps[:, 4 + k, j * D + c * P:j * D + (c + 1) * P],
                                            w2s[:, c, tile(2 * k + j)], ident[:])
                last.then_inc(signs_turned, 1)
            pe.wait_ge(diag_set, C)
            pe.wait_ge(sgn1_set, 3)
            for c in range(C):
                last = pe.matmul(ps[:, 2, c * P:(c + 1) * P], ones[:], diag[:, c, :], start=True, stop=True)
            last.then_inc(alpha2_spread, 1)
            scores(0, 0)
            pe.wait_ge(alpha2_set, 1)
            pe.wait_ge(sgn2_set, J // 2)

            def batch(i, s, more):
                b = 2 * i + s
                scores(b, 1)
                turn_probs(b, 0)
                for q in range(T - 2):
                    scores(b, q + 2)
                    turn_probs(b, q + 1)
                    weigh_values(b, q)
                if more:
                    turn_rows(b + 1, 0)
                turn_probs(b, T - 1)
                if more:
                    turn_rows(b + 1, 1)
                weigh_values(b, T - 2)
                weigh_values(b, T - 1)
                if more:
                    queries(b + 1, False)
                for n in range(N2):
                    pe.wait_ge(xn2_set, T * b + TH * (n + 1))
                    if more:
                        pe.wait_ge(km_set, N2 * (b + 1) + n + 1)
                    for t in range(TH):
                        for c in range(C):
                            last = pe.transpose(ps[:, 2 * n + c, tile(t)], xn2[:, TH * n + t, tile(c)], ident[:])
                    last.then_inc(x2_turned, 1)
                if more:
                    values(b + 1)
                for j in range(J):
                    if j == 0:
                        pe.wait_ge(x2l_set, N2 * (b + 1))
                    if j == 1 and more:
                        pe.wait_ge(vl_set, VG * (b + 1) + 2)
                    if j >= 2:
                        pe.wait_ge(gelu_set, J * b + j - 1)
                    for c in range(C):
                        for part in (x2h, x2l):
                            for n in range(N2):
                                last = pe.matmul(ps[:, 2 + 2 * (j % 2) + n, :], sgn1[:, c, tile(j)], part[:, c, half(n)],
                                                 start=c == 0 and part is x2h, stop=c == C - 1 and part is x2l)
                    last.then_inc(hidden, 1)
                if more:
                    scores(b + 1, 0)
                for t in range(T):
                    if t < 2 and more:
                        pe.wait_ge(vl_set, VG * (b + 1) + 3 + t)
                    if t >= 2:
                        pe.wait_ge(ffn_scaled, T * b + t - 1)
                    for j in range(J):
                        if t == 0:
                            pe.wait_ge(gl_set, J * b + j + 1)
                        pe.matmul(ps[:, OUT_BANK + t % 2, 0:D], gh[:, j, tile(t)], sgn2[:, j, :], start=j == 0, stop=False)
                        last = pe.matmul(ps[:, OUT_BANK + t % 2, 0:D], gl[:, j, tile(t)], sgn2[:, j, :],
                                         start=False, stop=j == J - 1)
                    last.then_inc(ffn_summed, 1)

            with pe.Fori(0, PAIRS - 1) as i:
                batch(i, 0, True)
                batch(i, 1, True)
            batch(PAIRS - 1, 0, True)
            batch(PAIRS - 1, 1, False)


_INS = ["L0_attn_x", "L0_attn_Wq", "L0_attn_bq", "L0_attn_Wk", "L0_attn_bk", "L0_attn_Wv", "L0_attn_bv",
        "L0_attn_Wo", "L0_attn_bo", "L0_ffn_w1", "L0_ffn_b1", "L0_ffn_w2", "L0_ffn_b2"]


def kernel(**inputs):
    import numpy as _np
    import concourse.bacc as _bacc
    from concourse import mybir as _mybir
    from concourse.bass_utils import run_bass_kernel_spmd as _run

    nc = _bacc.Bacc("TRN2", target_bir_lowering=False, num_devices=1)
    arrays, args = {}, []
    for name in _INS:
        a = _np.ascontiguousarray(inputs[name])
        arrays[f"in_{name}_dram"] = a
        args.append(nc.dram_tensor(f"in_{name}_dram", a.shape, _mybir.dt.from_np(a.dtype), kind="ExternalInput").ap())
    shape = tuple(inputs["L0_attn_x"].shape)
    mask = gaussian_mask_row(shape[1], shape[1] // P)
    arrays["mask_dram"] = mask
    args.append(nc.dram_tensor("mask_dram", mask.shape, _mybir.dt.from_np(mask.dtype), kind="ExternalInput").ap())
    args.append(nc.dram_tensor("out_dram", shape, F32, kind="ExternalOutput").ap())
    preln_attention_ffn(nc, *args)
    r = _run(nc, [arrays], core_ids=[0])
    return r.results[0]["out_dram"]
```

```python
from contextlib import ExitStack

import numpy as np
import concourse.bass as bass
from concourse import mybir

F32 = mybir.dt.float32
F32R = mybir.dt.float32r
ACT = mybir.ActivationFunctionType
ALU = mybir.AluOpType
AX_X = mybir.AxisListType.X

P = 128
HALF = 512
EPS = 1e-5
WARM_UP = 4
G_SLOTS = 3


def gaussian_mask_row(seq, tiles):
    pos = np.arange(seq, dtype=np.float32)
    mask = np.exp(np.float32(-0.5) * ((pos - np.float32(seq / 2)) / np.float32(seq / 4)) ** 2)
    return np.ascontiguousarray(mask.astype(np.float32).reshape(P, tiles).T).reshape(-1)


def preln_attention_ffn(nc, x, Wq, bq, Wk, bk, Wv, bv, Wo, bo, w1, b1, w2, b2, mask, out):
    B, S, D = x.shape
    H = w1.shape[0]
    T = S // P
    C = D // P
    J = H // P
    N2 = S // HALF
    TH = T // N2
    PAIRS = B // 2
    QG = C * N2
    VG = T // 2
    SCALE = float(D) ** -0.5

    x_v = x.rearrange("b (p t) d -> b p t d", t=T)
    out_v = out.rearrange("b (p t) d -> b p t d", t=T)

    with ExitStack() as ctx:
        def sb(name, shape, dt=F32, stack=ctx):
            return stack.enter_context(nc.sbuf_tensor(name, shape, dt))

        def sem(name):
            return ctx.enter_context(nc.semaphore(name))

        ident = sb("ident", [P, P])
        ones = sb("ones", [P, P])
        mask_bc = sb("mask_bc", [P, S])
        bias_bc = sb("bias_bc", [P, D])
        b2_bc = sb("b2_bc", [P, D])
        alpha2_bc = sb("alpha2_bc", [P, D])
        alpha1 = sb("alpha1", [P, J])
        alpha2 = sb("alpha2", [P, C])
        cols = sb("cols", [P, J + 3 * C])
        ccol = sb("ccol", [P, C])
        wkt = sb("wkt", [P, C])
        Mh = sb("Mh", [P, C, D], F32R)
        Ml = sb("Ml", [P, C, D], F32R)
        Nh = sb("Nh", [P, C, D], F32R)
        Nl = sb("Nl", [P, C, D], F32R)
        sgn1 = sb("sgn1", [P, C, H], F32R)
        sgn2 = sb("sgn2", [P, J, D], F32R)
        xin = [sb(f"xin{s}", [P, T, D]) for s in range(2)]
        kh = sb("kh", [P, C, S], F32R)
        kl = sb("kl", [P, C, S], F32R)
        qh = sb("qh", [P, C, S], F32R)
        ql = sb("ql", [P, C, S], F32R)
        vhl = sb("vhl", [P, T, 2, D], F32R)
        vh, vl = vhl[:, :, 0, :], vhl[:, :, 1, :]
        g = sb("g", [P, G_SLOTS, S])
        sw2 = g[:, 0:C, 0:H]
        ys = sb("ys", [P, 2, D])
        mhalf = sb("mhalf", [P, T])
        eps = sb("eps", [P, T])
        st1 = sb("st1", [P, T, 6])
        mv1 = sb("mv1", [P, T, 2])
        ve1 = sb("ve1", [P, T])
        rstd1 = sb("rstd1", [P, T])
        st2 = sb("st2", [P, T, 6])
        mv2 = sb("mv2", [P, T, 2])
        ve2 = sb("ve2", [P, T])
        rstd2 = sb("rstd2", [P, T])
        nmax = sb("nmax", [P, T])
        rsum = sb("rsum", [P, T])
        rinv = sb("rinv", [P, T])
        spare = sb("spare", [P, 1])

        with ExitStack() as place:
            xn1 = sb("xn1", [P, T, D], F32, place)
            xn2 = sb("xn2", [P, T, D], F32, place)
        with ExitStack() as place:
            x2h = sb("x2h", [P, C, S], F32R, place)
            x2l = sb("x2l", [P, C, S], F32R, place)
            with ExitStack() as inner:
                xh = sb("xh", [P, C, S], F32R, inner)
                xl = sb("xl", [P, C, S], F32R, inner)
                kmf = sb("kmf", [P, C, S], F32, inner)
                prob = sb("prob", [P, 2, S], F32, inner)
                pth = sb("pth", [P, 2, S], F32R, inner)
                ptl = sb("ptl", [P, 2, S], F32R, inner)
            with ExitStack() as inner:
                sb("gap", [P, 3 * C * S], F32, inner)
                wq = sb("wq", [P, C, D], F32, inner)
                wk = sb("wk", [P, C, D], F32, inner)
                wv = sb("wv", [P, C, D], F32, inner)
                wo = sb("wo", [P, C, D], F32, inner)
                wkc = sb("wkc", [P, C, D], F32, inner)
                woT = sb("woT", [P, C, D], F32, inner)
                w1s = sb("w1s", [P, J, D], F32, inner)
                w2s = sb("w2s", [P, C, H], F32, inner)
                sw1 = sb("sw1", [P, J, D], F32, inner)
                rows = sb("rows", [J + 3 * C, P], F32, inner)
                bvb = sb("bvb", [P, C, P], F32, inner)
                diag = sb("diag", [P, C, P], F32, inner)
            gh = sb("gh", [P, J, S], F32R, place)
            gl = sb("gl", [P, J, S], F32R, place)

        ps = ctx.enter_context(nc.psum_tensor("ps", [P, 8, HALF], F32))
        PT_BANK, OUT_BANK = 4, 6

        first_loaded = sem("first_loaded")
        x_loaded = [sem(f"x_loaded{s}") for s in range(2)]
        wqk_loaded, wvo_loaded, w1_loaded, w2_loaded, rows_loaded, bcast_loaded = (
            sem(n) for n in ("wqk_loaded", "wvo_loaded", "w1_loaded", "w2_loaded", "rows_loaded", "bcast_loaded"))
        consts_set, rows_turned, cols_set, wkc_set, m_summed, mh_set, ml_set, c_summed, ccol_set = (
            sem(n) for n in ("consts_set", "rows_turned", "cols_set", "wkc_set", "m_summed", "mh_set", "ml_set",
                             "c_summed", "ccol_set"))
        wo_turned, woT_set, bvb_set, n_summed, nh_set, nl_set, bias_summed, bias_set = (
            sem(n) for n in ("wo_turned", "woT_set", "bvb_set", "n_summed", "nh_set", "nl_set", "bias_summed",
                             "bias_set"))
        alphas_set, diag_set, alpha2_spread, alpha2_set, neg_set, signs_set, signs_turned, sgn1_set, sgn2_set = (
            sem(n) for n in ("alphas_set", "diag_set", "alpha2_spread", "alpha2_set", "neg_set", "signs_set",
                             "signs_turned", "sgn1_set", "sgn2_set"))
        y_stored = sem("y_stored")
        stats1, aggr1, vareps1, rstd1_set, xn1_set, xbias_added = (
            sem(n) for n in ("stats1", "aggr1", "vareps1", "rstd1_set", "xn1_set", "xbias_added"))
        x_turned, xh_set, xl_set, km_set, kh_set, kl_set = (
            sem(n) for n in ("x_turned", "xh_set", "xl_set", "km_set", "kh_set", "kl_set"))
        q_summed, qh_set, ql_set, v_summed, vh_set, vl_set = (
            sem(n) for n in ("q_summed", "qh_set", "ql_set", "v_summed", "vh_set", "vl_set"))
        scored, max_set, exp_set, p_turned, pth_set, ptl_set, rinv_set, pv_summed, x1_half, x1_set = (
            sem(n) for n in ("scored", "max_set", "exp_set", "p_turned", "pth_set", "ptl_set", "rinv_set",
                             "pv_summed", "x1_half", "x1_set"))
        stats2, aggr2, vareps2, rstd2_set, xn2_set, b2_added = (
            sem(n) for n in ("stats2", "aggr2", "vareps2", "rstd2_set", "xn2_set", "b2_added"))
        x2_turned, x2h_set, x2l_set, hidden, gelu_set, gh_set, gl_set = (
            sem(n) for n in ("x2_turned", "x2h_set", "x2l_set", "hidden", "gelu_set", "gh_set", "gl_set"))
        ffn_summed, ffn_scaled, y_set, table_loaded = (
            sem(n) for n in ("ffn_summed", "ffn_scaled", "y_set", "table_loaded"))

        block = ctx.enter_context(nc.Block())

        def slot(s):
            return ps[:, 2 * s:2 * s + 2, :]

        def two(ap):
            return ap.rearrange("p (a n) -> p a n", a=2)

        def half(n):
            return slice(n * HALF, (n + 1) * HALF)

        def tile(t):
            return slice(t * P, (t + 1) * P)

        def pair_of(k):
            n, m = divmod(k, J // 2)
            return n, slice(2 * m, 2 * m + 2)


        @block.sync
        def _(sp):
            sp.dma_start(xin[0][:, 0:TH, :], x_v[0, :, 0:TH, :]).then_inc(first_loaded, 16)
            sp.dma_start(xin[0][:, TH:T, :], x_v[0, :, TH:T, :]).then_inc(x_loaded[0], 16)
            sp.dma_start(wk[:], Wk.rearrange("(c p) d -> p c d", p=P)).then_inc(wqk_loaded, 16)
            sp.dma_start(wq[:], Wq.rearrange("(c p) d -> p c d", p=P)).then_inc(wqk_loaded, 16)
            sp.dma_start(wo[:], Wo.rearrange("(c p) d -> p c d", p=P)).then_inc(wvo_loaded, 16)
            sp.dma_start(wv[:], Wv.rearrange("(c p) d -> p c d", p=P)).then_inc(wvo_loaded, 16)
            sp.dma_start(bias_bc[:], bo.partition_broadcast(P)).then_inc(bcast_loaded, 16)
            sp.dma_start(mask_bc[:], mask.partition_broadcast(P)).then_inc(bcast_loaded, 16)
            sp.dma_start(b2_bc[:], b2.partition_broadcast(P)).then_inc(bcast_loaded, 16)
            sp.dma_start(w1s[:], w1.rearrange("(j p) d -> p j d", p=P)).then_inc(w1_loaded, 16)
            sp.dma_start(w2s[:], w2.rearrange("(c p) h -> p c h", p=P)).then_inc(w2_loaded, 16)
            sp.dma_start(xin[1][:], x_v[1]).then_inc(x_loaded[1], 16)

            def store_and_load(i, s, more):
                b = 2 * i + s
                for n in range(N2):
                    sp.wait_ge(y_set, T * b + TH * (n + 1))
                    sp.dma_start(out_v[b, :, n * TH:(n + 1) * TH, :],
                                 xin[s][:, n * TH:(n + 1) * TH, :]).then_inc(y_stored, 16)
                if more:
                    sp.wait_ge(y_stored, 16 * N2 * (b + 1))
                    sp.dma_start(xin[s][:], x_v[b + 2]).then_inc(x_loaded[s], 16)

            with sp.Fori(0, PAIRS - 1) as i:
                store_and_load(i, 0, True)
                store_and_load(i, 1, True)
            store_and_load(PAIRS - 1, 0, False)
            store_and_load(PAIRS - 1, 1, False)
            sp.wait_ge(y_stored, 16 * N2 * B)

        @block.gpsimd
        def _(pool):
            pool.memset(ident[:], 0.0).then_inc(consts_set, 1)
            pool.memset(ones[:], 1.0).then_inc(consts_set, 1)
            pool.memset(mhalf[:], -0.5).then_inc(consts_set, 1)
            pool.memset(eps[:], EPS).then_inc(consts_set, 1)
            pool.wait_ge(consts_set, 4)
            pool.affine_select(out=ident[:], in_=ident[:], compare_op=ALU.not_equal, fill=1.0, base=0,
                               pattern=[[-1, P]], channel_multiplier=1).then_inc(consts_set, 1)

            def rstd_attention(b):
                pool.wait_ge(aggr1, T * (b + 1))
                pool.tensor_tensor(ve1[:], mv1[:, :, 1], eps[:], ALU.add).then_inc(vareps1, 1)
                pool.wait_ge(vareps1, b + 1)
                pool.tensor_tensor(rstd1[:], ve1[:], mhalf[:], ALU.pow).then_inc(rstd1_set, 1)

            def rstd_ffn(b, q):
                pool.wait_ge(aggr2, T * b + q + 1)
                pool.tensor_tensor(ve2[:, q:q + 1], mv2[:, q, 1:2], eps[:, q:q + 1], ALU.add).then_inc(vareps2, 1)
                pool.wait_ge(vareps2, T * b + q + 1)
                pool.tensor_tensor(rstd2[:, q:q + 1], ve2[:, q:q + 1], mhalf[:, q:q + 1],
                                   ALU.pow).then_inc(rstd2_set, 1)

            def split_keys(b):
                for n in range(N2):
                    pool.wait_ge(kh_set, N2 * b + n + 1)
                    pool.tensor_tensor(kl[:, :, half(n)], kmf[:, :, half(n)],
                                       kh[:, :, half(n)].bitcast(F32), ALU.subtract).then_inc(kl_set, 1)

            def add_bias(b, s, t):
                if t == 0:
                    pool.wait_ge(xn1_set, T * (b + 1))
                pool.tensor_tensor(xin[s][:, t, :], xin[s][:, t, :], bias_bc[:], ALU.add).then_inc(xbias_added, 1)

            rstd_attention(0)
            split_keys(0)
            pool.wait_ge(bias_set, 1)
            for t in range(T):
                add_bias(0, 0, t)

            def batch(i, s, more):
                b = 2 * i + s
                for q in range(TH):
                    rstd_ffn(b, q)
                if more:
                    rstd_attention(b + 1)
                for q in range(TH, T):
                    rstd_ffn(b, q)
                if more:
                    split_keys(b + 1)
                for j in range(J):
                    if j == 0:
                        pool.wait_ge(xn2_set, T * (b + 1))
                    pool.tensor_tensor(xin[s][:, j, :], xin[s][:, j, :], b2_bc[:], ALU.add).then_inc(b2_added, 1)
                for t in range(T):
                    if t == 0:
                        pool.wait_ge(b2_added, T * (b + 1))
                    pool.wait_ge(ffn_scaled, T * b + t + 1)
                    pool.tensor_tensor(xin[s][:, t, :], xin[s][:, t, :], ys[:, t % 2, :], ALU.add).then_inc(y_set, 1)
                    if more:
                        add_bias(b + 1, 1 - s, t)

            with pool.Fori(0, PAIRS - 1) as i:
                batch(i, 0, True)
                batch(i, 1, True)
            batch(PAIRS - 1, 0, True)
            batch(PAIRS - 1, 1, False)

        @block.scalar
        def _(act):
            act.dma_start(rows[0:J, :], b1.rearrange("(j p) -> j p", p=P)).then_inc(rows_loaded, 16)
            for n, b_dram in enumerate((bq, bk, bv)):
                act.dma_start(rows[J + C * n:J + C * (n + 1), :],
                              b_dram.rearrange("(c p) -> c p", p=P)).then_inc(rows_loaded, 16)

            def hi_rows(b, n):
                act.wait_ge(x_turned, N2 * b + n + 1)
                act.activation(xh[:, :, half(n)], slot(n), ACT.Copy).then_inc(xh_set, 1)

            def hi_queries(b):
                for k in range(QG):
                    n, m = divmod(k, C)
                    act.wait_ge(q_summed, QG * b + k + 1)
                    act.activation(qh[:, m, half(n)], ps[:, PT_BANK + k, :], ACT.Identity,
                                   bias=ccol[:, m:m + 1]).then_inc(qh_set, 1)

            def hi_values(b):
                for k in range(VG):
                    act.wait_ge(v_summed, VG * b + k + 1)
                    act.activation(vh[:, 2 * k:2 * k + 2], two(ps[:, PT_BANK + k, :]), ACT.Copy).then_inc(vh_set, 1)

            def hi_keys(b):
                for n in range(N2):
                    act.wait_ge(km_set, N2 * b + n + 1)
                    act.activation(kh[:, :, half(n)], kmf[:, :, half(n)], ACT.Copy).then_inc(kh_set, 1)

            act.wait_ge(wo_turned, 1)
            act.activation(woT[:].rearrange("p c d -> p (c d)"), ps[:, 2, :], ACT.Copy).then_inc(woT_set, 1)
            act.wait_ge(m_summed, 1)
            act.activation(Mh[:].rearrange("p c d -> p (c d)"), ps[:, 4, :], ACT.Copy, scale=SCALE).then_inc(mh_set, 1)
            for n in range(N2):
                hi_rows(0, n)
            act.wait_ge(n_summed, 1)
            act.activation(Nh[:].rearrange("p c d -> p (c d)"), ps[:, 7, :], ACT.Copy).then_inc(nh_set, 1)
            act.wait_ge(w2_loaded, 16)
            for c in range(C):
                act.activation(prob[:, c, 0:H], w2s[:, c, :], ACT.Abs, scale=1.0 / H,
                               accum_out=alpha2[:, c:c + 1]).then_inc(alphas_set, 1)
            act.wait_ge(ccol_set, 1)
            hi_queries(0)
            hi_keys(0)
            hi_values(0)
            for k in range(2 * C):
                c, n = divmod(k, 2)
                act.wait_ge(signs_turned, k + 1)
                act.activation(sgn1[:, c, half(n)], ps[:, k, :], ACT.Copy).then_inc(sgn1_set, 1)
            act.wait_ge(w1_loaded, 16)
            act.wait_ge(alphas_set, C)
            for j in range(J):
                act.activation(prob[:].rearrange("p a s -> p (a s)")[:, j * D:(j + 1) * D], w1s[:, j, :], ACT.Abs,
                               scale=1.0 / D, accum_out=alpha1[:, j:j + 1]).then_inc(alphas_set, 1)
            for k in range(J // 2):
                act.wait_ge(signs_turned, 2 * C + k + 1)
                act.activation(sgn2[:, 2 * k:2 * k + 2, :], two(ps[:, 4 + k, :]), ACT.Copy).then_inc(sgn2_set, 1)

            act.wait_ge(alphas_set, C + J)

            def exponentials(b, q):
                act.wait_ge(max_set, T * b + q + 1)
                if q == 0:
                    act.wait_ge(ffn_summed, T * b + 1)
                act.activation(two(prob[:, q % 2, :]), slot(q % 2), ACT.Exp, bias=nmax[:, q:q + 1],
                               accum_out=rsum[:, q:q + 1]).then_inc(exp_set, 1)

            def hi_probs(b, q):
                act.wait_ge(p_turned, T * b + q + 1)
                act.activation(two(pth[:, q % 2, :]), ps[:, PT_BANK:PT_BANK + 2, :], ACT.Copy).then_inc(pth_set, 1)

            def hi_rows_ffn(b, n, banks):
                act.wait_ge(x2_turned, N2 * b + n + 1)
                act.activation(x2h[:, :, half(n)], banks, ACT.Copy).then_inc(x2h_set, 1)

            def load_table(b, func):
                if func == ACT.Exp:
                    act.wait_ge(table_loaded, 2 * b + 1)
                act.activation(spare[:], eps[:, 0:1], func).then_inc(table_loaded, 1)

            def hidden_ready(b, k):
                act.wait_ge(hidden, J * b + k + 1)
                if k >= G_SLOTS:
                    act.wait_ge(gl_set, J * b + k - G_SLOTS + 1)

            def last_ffn(b):
                hi_rows_ffn(b, 0, slot(0))
                load_table(b, ACT.Gelu)
                for k in range(J):
                    n, js = pair_of(k)
                    if k == J // 2 - 2:
                        hi_rows_ffn(b, 1, slot(0))
                    hidden_ready(b, k)
                    for m, j in enumerate(range(js.start, js.stop)):
                        last = act.activation(g[:, k % G_SLOTS, half(m)], ps[:, 2 + 2 * (k % 2) + m, :], ACT.Gelu,
                                              bias=cols[:, j:j + 1], scale=alpha1[:, j:j + 1])
                    last.then_inc(gelu_set, 1)

            def batch(i, s, more):
                b = 2 * i + s
                exponentials(b, 0)
                for q in range(T - 1):
                    hi_probs(b, q)
                    exponentials(b, q + 1)
                if more:
                    hi_rows(b + 1, 0)
                hi_probs(b, T - 1)
                if not more:
                    last_ffn(b)
                    return
                hi_rows(b + 1, 1)
                hi_queries(b + 1)
                hi_keys(b + 1)
                for n in range(N2):
                    hi_rows_ffn(b, n, slot(n))
                load_table(b, ACT.Gelu)
                hi_values(b + 1)
                for j in range(J):
                    hidden_ready(b, j)
                    act.activation(two(g[:, j % G_SLOTS, :]), slot(1 + j % 2), ACT.Gelu, bias=cols[:, j:j + 1],
                                   scale=alpha1[:, j:j + 1]).then_inc(gelu_set, 1)
                load_table(b, ACT.Exp)

            with act.Fori(0, PAIRS - 1) as i:
                batch(i, 0, True)
                batch(i, 1, True)
            batch(PAIRS - 1, 0, True)
            batch(PAIRS - 1, 1, False)

        @block.vector
        def _(dve):
            def stats_attention(s, tiles):
                for t in tiles:
                    dve.bn_stats(st1[:, t, :], xin[s][:, t, :]).then_inc(stats1, 1)

            def aggregate_attention(b):
                for t in range(T):
                    dve.bn_aggr(mv1[:, t, :], st1[:, t, :]).then_inc(aggr1, 1)

            def normalize_attention(b, s, tiles):
                for t in tiles:
                    if t == 0:
                        dve.wait_ge(rstd1_set, b + 1)
                    dve.tensor_scalar(xn1[:, t, :], xin[s][:, t, :], mv1[:, t, 0:1], rstd1[:, t:t + 1],
                                      ALU.subtract, ALU.mult).then_inc(xn1_set, 1)

            def lo_rows(b, n):
                dve.wait_ge(xh_set, N2 * b + n + 1)
                dve.tensor_tensor(xl[:, :, half(n)], slot(n), xh[:, :, half(n)].bitcast(F32),
                                  ALU.subtract).then_inc(xl_set, 1)

            def mask_keys(b, n):
                m = mask_bc[:, half(n)].unsqueeze(1).broadcast_to([P, C, HALF])
                dve.scalar_tensor_tensor(out=kmf[:, :, half(n)], in0=slot(n), scalar=1.0, in1=m,
                                         op0=ALU.add, op1=ALU.mult).then_inc(km_set, 1)

            def lo_queries(b, groups):
                for k in groups:
                    n, m = divmod(k, C)
                    dve.wait_ge(qh_set, QG * b + k + 1)
                    dve.scalar_tensor_tensor(out=ql[:, m, half(n)], in0=ps[:, PT_BANK + k, :], scalar=ccol[:, m:m + 1],
                                             in1=qh[:, m, half(n)].bitcast(F32), op0=ALU.add,
                                             op1=ALU.subtract).then_inc(ql_set, 1)

            def lo_values(b):
                for k in range(VG):
                    dve.wait_ge(vh_set, VG * b + k + 1)
                    dve.tensor_tensor(vl[:, 2 * k:2 * k + 2], two(ps[:, PT_BANK + k, :]),
                                      vh[:, 2 * k:2 * k + 2].bitcast(F32), ALU.subtract).then_inc(vl_set, 1)

            def row_max(b, q):
                dve.wait_ge(scored, T * b + q + 1)
                dve.tensor_reduce(nmax[:, q:q + 1], slot(q % 2), mybir.AxisListType.XY, ALU.max,
                                  negate=True).then_inc(max_set, 1)

            def lo_probs(b, q):
                dve.wait_ge(pth_set, T * b + q + 1)
                dve.tensor_tensor(two(ptl[:, q % 2, :]), ps[:, PT_BANK:PT_BANK + 2, :],
                                  two(pth[:, q % 2, :].bitcast(F32)), ALU.subtract).then_inc(ptl_set, 1)

            def invert_sum(q):
                dve.reciprocal(rinv[:, q:q + 1], rsum[:, q:q + 1]).then_inc(rinv_set, 1)

            def add_attention(b, s, q):
                dve.wait_ge(pv_summed, T * b + q + 1)
                dve.wait_ge(rinv_set, T * b + q + 1)
                dve.wait_ge(xbias_added, T * b + q + 1)
                dve.scalar_tensor_tensor(out=xin[s][:, q, :], in0=ps[:, OUT_BANK + q % 2, D:2 * D], scalar=rinv[:, q:q + 1],
                                         in1=xin[s][:, q, :], op0=ALU.mult, op1=ALU.add).then_inc(x1_half, 1)
                dve.wait_ge(x1_half, T * b + q + 1)
                dve.scalar_tensor_tensor(out=xin[s][:, q, :], in0=ps[:, OUT_BANK + q % 2, 0:D], scalar=rinv[:, q:q + 1],
                                         in1=xin[s][:, q, :], op0=ALU.mult, op1=ALU.add).then_inc(x1_set, 1)
                dve.wait_ge(x1_set, T * b + q + 1)
                dve.bn_stats(st2[:, q, :], xin[s][:, q, :]).then_inc(stats2, 1)
                dve.wait_ge(stats2, T * b + q + 1)
                if q < T - 1:
                    invert_sum(q + 1)
                else:
                    normalize_ffn(b, s, q - 1)
                dve.bn_aggr(mv2[:, q, :], st2[:, q, :]).then_inc(aggr2, 1)

            def normalize_ffn(b, s, q):
                dve.wait_ge(rstd2_set, T * b + q + 1)
                dve.tensor_scalar(xn2[:, q, :], xin[s][:, q, :], mv2[:, q, 0:1], rstd2[:, q:q + 1],
                                  ALU.subtract, ALU.mult).then_inc(xn2_set, 1)

            def lo_rows_ffn(b, n, part, banks):
                dve.wait_ge(x2h_set, N2 * b + n + 1)
                dve.tensor_tensor(part[:, :, half(n)], banks, x2h[:, :, half(n)].bitcast(F32),
                                  ALU.subtract).then_inc(x2l_set, 1)

            def split_hidden(b, k, hi, lo):
                dve.wait_ge(gelu_set, J * b + k + 1)
                dve.tensor_copy(hi, two(g[:, k % G_SLOTS, :])).then_inc(gh_set, 1)
                dve.wait_ge(gh_set, J * b + k + 1)
                dve.tensor_tensor(lo, two(g[:, k % G_SLOTS, :]), hi.bitcast(F32), ALU.subtract).then_inc(gl_set, 1)

            def scale_outputs(b, tiles):
                for t in tiles:
                    dve.wait_ge(ffn_summed, T * b + t + 2)
                    if t >= 2:
                        dve.wait_ge(y_set, T * b + t - 1)
                    dve.tensor_tensor(ys[:, t % 2, :], ps[:, OUT_BANK + t % 2, 0:D], alpha2_bc[:],
                                      ALU.mult).then_inc(ffn_scaled, 1)

            def last_ffn(b, s):
                normalize_ffn(b, s, T - 3)
                add_attention(b, s, T - 2)
                lo_rows_ffn(b, 0, kl, slot(0))
                add_attention(b, s, T - 1)
                normalize_ffn(b, s, T - 1)
                for k in range(J):
                    n, js = pair_of(k)
                    if k == J // 2 - 2:
                        lo_rows_ffn(b, 1, kl, slot(0))
                    if k == J - 1:
                        scale_outputs(b, range(1))
                    split_hidden(b, k, gh[:, js, half(n)], gl[:, js, half(n)])
                scale_outputs(b, range(1, T))

            dve.wait_ge(first_loaded, 16)
            stats_attention(0, range(TH))
            dve.wait_ge(x_loaded[0], 16)
            stats_attention(0, range(TH, T))
            dve.wait_ge(stats1, T)
            aggregate_attention(0)
            dve.wait_ge(rows_turned, 1)
            dve.tensor_copy(cols[:], ps[:, 3, 0:J + 3 * C]).then_inc(cols_set, 1)
            dve.wait_ge(wqk_loaded, 32)
            dve.tensor_reduce(wkt[:], wk[:], AX_X, ALU.add).then_inc(wkc_set, 1)
            dve.wait_ge(cols_set, 1)
            dve.wait_ge(wkc_set, 1)
            bk_c, bv_c = (cols[:, J + C * n:J + C * (n + 1)] for n in (1, 2))
            dve.tensor_tensor(wkt[:], bk_c, wkt[:], ALU.subtract).then_inc(wkc_set, 1)
            dve.wait_ge(wkc_set, 2)
            for c in range(C):
                dve.scalar_tensor_tensor(out=wkc[:, c, :], in0=wkt[:, c:c + 1].broadcast_to([P, D]), scalar=1.0 / D,
                                         in1=wk[:, c, :], op0=ALU.mult, op1=ALU.add).then_inc(wkc_set, 1)
            for c in range(C):
                dve.tensor_scalar(bvb[:, c, :], ones[:], bv_c[:, c:c + 1], None, ALU.mult).then_inc(bvb_set, 1)
            normalize_attention(0, 0, range(T))
            dve.wait_ge(mh_set, 1)
            dve.scalar_tensor_tensor(out=Ml[:].rearrange("p c d -> p (c d)"), in0=ps[:, 4, :], scalar=SCALE,
                                     in1=Mh[:].rearrange("p c d -> p (c d)").bitcast(F32), op0=ALU.mult,
                                     op1=ALU.subtract).then_inc(ml_set, 1)
            for n in range(N2):
                lo_rows(0, n)
            dve.wait_ge(nh_set, 1)
            dve.tensor_tensor(Nl[:].rearrange("p c d -> p (c d)"), ps[:, 7, :],
                              Nh[:].rearrange("p c d -> p (c d)").bitcast(F32), ALU.subtract).then_inc(nl_set, 1)
            dve.wait_ge(bias_summed, 1)
            dve.wait_ge(bcast_loaded, 16 * 3)
            dve.tensor_tensor(bias_bc[:], ps[:, 6, 0:D], bias_bc[:], ALU.add).then_inc(bias_set, 1)
            dve.wait_ge(c_summed, 1)
            dve.tensor_scalar(ccol[:], ps[:, 5, 0:C], SCALE, None, ALU.mult).then_inc(ccol_set, 1)
            def negatives(sign, w):
                dve.tensor_scalar(sign[:], w[:], 0.0, None, ALU.is_lt).then_inc(neg_set, 1)

            def signs(n, sign, w):
                dve.wait_ge(neg_set, n + 1)
                dve.scalar_tensor_tensor(out=sign[:], in0=w[:], scalar=0.0, in1=sign[:], op0=ALU.is_gt,
                                         op1=ALU.subtract).then_inc(signs_set, 1)

            dve.wait_ge(w1_loaded, 16)
            negatives(sw1, w1s)
            mask_keys(0, 0)
            lo_queries(0, range(1))
            mask_keys(0, 1)
            dve.wait_ge(alphas_set, C)
            for c in range(C):
                dve.tensor_scalar(diag[:, c, :], ident[:], alpha2[:, c:c + 1], None, ALU.mult).then_inc(diag_set, 1)
            lo_queries(0, range(1, QG))
            dve.wait_ge(alpha2_spread, 1)
            dve.tensor_copy(alpha2_bc[:], ps[:, 0, 0:D]).then_inc(alpha2_set, 1)
            signs(0, sw1, w1s)
            dve.wait_ge(w2_loaded, 16)
            negatives(sw2, w2s)
            lo_values(0)
            signs(1, sw2, w2s)
            row_max(0, 0)

            def batch(i, s, more):
                b = 2 * i + s
                r, loads = 1 - s, i + 1 + s
                row_max(b, 1)
                lo_probs(b, 0)
                invert_sum(0)
                for q in range(T - 2):
                    if q == 4 and more:
                        dve.wait_ge(stats1, T * (b + 2))
                    if q == 5 and more:
                        normalize_attention(b + 1, r, range(TH))
                    row_max(b, q + 2)
                    lo_probs(b, q + 1)
                    if q == 5 and more:
                        normalize_attention(b + 1, r, range(TH, T))
                    if q >= 1:
                        normalize_ffn(b, s, q - 1)
                    if more:
                        if q == 2:
                            dve.wait_ge(x_loaded[r], 16 * loads)
                            stats_attention(r, range(TH))
                        if q == 3:
                            stats_attention(r, range(TH, T))
                        if q == 4:
                            aggregate_attention(b + 1)
                    add_attention(b, s, q)
                lo_probs(b, T - 1)
                if not more:
                    last_ffn(b, s)
                    return
                lo_rows(b + 1, 0)
                normalize_ffn(b, s, T - 3)
                lo_rows(b + 1, 1)
                add_attention(b, s, T - 2)
                mask_keys(b + 1, 0)
                add_attention(b, s, T - 1)
                mask_keys(b + 1, 1)
                normalize_ffn(b, s, T - 1)
                lo_queries(b + 1, range(QG))
                dve.wait_ge(x2_turned, N2 * (b + 1))
                for n in range(N2):
                    lo_rows_ffn(b, n, x2l, slot(n))
                lo_values(b + 1)
                dve.wait_ge(kl_set, N2 * (b + 2))
                for j in range(J):
                    split_hidden(b, j, two(gh[:, j, :]), two(gl[:, j, :]))
                row_max(b + 1, 0)
                scale_outputs(b, range(T))

            with dve.Fori(0, PAIRS - 1) as i:
                batch(i, 0, True)
                batch(i, 1, True)
            batch(PAIRS - 1, 0, True)
            batch(PAIRS - 1, 1, False)

        @block.tensor
        def _(pe):
            def turn_rows(b, n):
                pe.wait_ge(xn1_set, T * b + TH * (n + 1))
                for t in range(TH):
                    for c in range(C):
                        last = pe.transpose(ps[:, 2 * n + c, tile(t)], xn1[:, TH * n + t, tile(c)], ident[:])
                last.then_inc(x_turned, 1)

            def queries(b, first):
                for k in range(QG):
                    n, m = divmod(k, C)
                    if m == 0:
                        pe.wait_ge(xl_set, N2 * b + n + 1)
                    if first and k == 1:
                        pe.wait_ge(ccol_set, 1)
                        pe.wait_ge(bias_set, 1)
                    if not first and k >= 2:
                        pe.wait_ge(x1_set, T * (b - 1) + T - 3 + k)
                    bank = ps[:, PT_BANK + k, :]
                    for c in range(C):
                        pe.matmul(bank, Mh[:, c, tile(m)], xh[:, c, half(n)], start=c == 0, stop=False)
                        pe.matmul(bank, Mh[:, c, tile(m)], xl[:, c, half(n)], start=False, stop=False)
                    for c in range(C):
                        last = pe.matmul(bank, Ml[:, c, tile(m)], xh[:, c, half(n)], start=False, stop=c == C - 1)
                    last.then_inc(q_summed, 1)

            def values(b):
                for k in range(VG):
                    pe.wait_ge(ql_set, QG * b + k + 1)
                    for t in range(2 * k, 2 * k + 2):
                        bank = ps[:, PT_BANK + k, (t % 2) * D:(t % 2 + 1) * D]
                        for c in range(C):
                            pe.matmul(bank, xh[:, c, tile(t)], Nh[:, c, :], start=c == 0, stop=False)
                            pe.matmul(bank, xh[:, c, tile(t)], Nl[:, c, :], start=False, stop=False)
                        for c in range(C):
                            last = pe.matmul(bank, xl[:, c, tile(t)], Nh[:, c, :], start=False, stop=c == C - 1)
                    last.then_inc(v_summed, 1)

            def scores(b, q):
                if q == 0:
                    pe.wait_ge(kl_set, N2 * (b + 1))
                    pe.wait_ge(ql_set, QG * (b + 1))
                for c in range(C):
                    for part, keys in ((qh, kh), (qh, kl), (ql, kh)):
                        for n in range(N2):
                            last = pe.matmul(ps[:, 2 * (q % 2) + n, :], part[:, c, tile(q)], keys[:, c, half(n)],
                                             start=c == 0 and part is qh and keys is kh,
                                             stop=c == C - 1 and part is ql)
                last.then_inc(scored, 1)

            def turn_probs(b, q):
                pe.wait_ge(exp_set, T * b + q + 1)
                if q >= 1:
                    pe.wait_ge(ptl_set, T * b + q)
                for t in range(T):
                    last = pe.transpose(ps[:, PT_BANK + t // TH, tile(t % TH)], prob[:, q % 2, tile(t)], ident[:])
                last.then_inc(p_turned, 1)

            def weigh_values(b, q):
                if q == 0:
                    pe.wait_ge(vl_set, VG * (b + 1))
                pe.wait_ge(ptl_set, T * b + q + 1)
                if q >= 2:
                    pe.wait_ge(x1_set, T * b + q - 1)
                bank = ps[:, OUT_BANK + q % 2, :]
                for t in range(T):
                    pe.matmul(bank, pth[:, q % 2, tile(t)], vhl[:, t, :, :], start=t == 0, stop=False)
                for t in range(T):
                    last = pe.matmul(bank[:, 0:D], ptl[:, q % 2, tile(t)], vh[:, t, :], start=False, stop=t == T - 1)
                last.then_inc(pv_summed, 1)

            def ffn_rows(b, t, chunks, by_chunk, more):
                if chunks[0] == 0:
                    if t < 2 and more:
                        pe.wait_ge(vl_set, VG * (b + 1) + 3 + t)
                    if t >= 2:
                        pe.wait_ge(ffn_scaled, T * b + t - 1)
                bank = ps[:, OUT_BANK + t % 2, 0:D]
                for j in chunks:
                    if by_chunk:
                        pe.wait_ge(gl_set, J * b + j + 1)
                    pe.matmul(bank, gh[:, j, tile(t)], sgn2[:, j, :], start=j == 0, stop=False)
                    last = pe.matmul(bank, gl[:, j, tile(t)], sgn2[:, j, :], start=False, stop=j == J - 1)
                if chunks[-1] == J - 1:
                    last.then_inc(ffn_summed, 1)

            def turn_rows_ffn(b, n, bank):
                pe.wait_ge(xn2_set, T * b + TH * (n + 1))
                for t in range(TH):
                    for c in range(C):
                        last = pe.transpose(ps[:, bank + c, tile(t)], xn2[:, TH * n + t, tile(c)], ident[:])
                last.then_inc(x2_turned, 1)

            def last_ffn(b):
                turn_rows_ffn(b, 0, 0)
                weigh_values(b, T - 1)
                for k in range(J):
                    n, js = pair_of(k)
                    if k == J // 2 - 2:
                        pe.wait_ge(x2l_set, N2 * b + 1)
                        turn_rows_ffn(b, 1, 0)
                    if k % (J // 2) == 0:
                        pe.wait_ge(x2l_set, N2 * b + n + 1)
                    if k >= 2:
                        pe.wait_ge(gelu_set, J * b + k - 1)
                    for m, j in enumerate(range(js.start, js.stop)):
                        for c in range(C):
                            for part in (x2h, kl):
                                last = pe.matmul(ps[:, 2 + 2 * (k % 2) + m, :], sgn1[:, c, tile(j)], part[:, c, half(n)],
                                                 start=c == 0 and part is x2h, stop=c == C - 1 and part is kl)
                    last.then_inc(hidden, 1)
                for t in range(T):
                    if t % TH == 0:
                        pe.wait_ge(gl_set, J * b + (J // 2) * (t // TH + 1))
                    ffn_rows(b, t, range(J), False, False)

            pe.wait_ge(consts_set, 5)
            for _ in range(WARM_UP):
                pe.matmul(ps[:, 0, :], ones[:], ones[:].unsqueeze(1).broadcast_to([P, HALF // P, P]), start=True, stop=True)
            pe.wait_ge(rows_loaded, 16 * 4)
            pe.transpose(ps[:, 3, 0:J + 3 * C], rows[:], ident[0:J + 3 * C, 0:J + 3 * C]).then_inc(rows_turned, 1)
            pe.wait_ge(wvo_loaded, 32)
            for e in range(C):
                for c in range(C):
                    last = pe.transpose(ps[:, 2, e * D + c * P:e * D + (c + 1) * P], wo[:, c, tile(e)], ident[:])
                if e == 0:
                    last.then_inc(ffn_summed, 1)
            last.then_inc(wo_turned, 1)
            pe.wait_ge(wqk_loaded, 32)
            pe.wait_ge(wkc_set, 2 + C)
            for m in range(C):
                for c in range(C):
                    last = pe.matmul(ps[:, 4, m * D:(m + 1) * D], wq[:, c, tile(m)], wkc[:, c, :],
                                     start=c == 0, stop=c == C - 1)
            last.then_inc(m_summed, 1)
            pe.wait_ge(woT_set, 1)
            pe.wait_ge(bvb_set, C)
            for n in range(N2):
                turn_rows(0, n)
            for m in range(C):
                for e in range(C):
                    last = pe.matmul(ps[:, 7, m * D:(m + 1) * D], wv[:, e, tile(m)], woT[:, e, :],
                                     start=e == 0, stop=e == C - 1)
            last.then_inc(n_summed, 1)
            for e in range(C):
                last = pe.matmul(ps[:, 6, 0:D], bvb[:, e, :], woT[:, e, :], start=e == 0, stop=e == C - 1)
            last.then_inc(bias_summed, 1)
            for m in range(C):
                for c in range(C):
                    last = pe.matmul(ps[:, 5, m:m + 1], wkc[:, c, tile(m)], cols[:, J + c:J + c + 1],
                                     start=c == 0, stop=c == C - 1)
            last.then_inc(c_summed, 1)

            pe.wait_ge(ml_set, 1)
            queries(0, True)
            pe.wait_ge(diag_set, C)
            pe.wait_ge(km_set, N2)
            for c in range(C):
                last = pe.matmul(ps[:, 0, c * P:(c + 1) * P], ones[:], diag[:, c, :], start=True, stop=True)
            last.then_inc(alpha2_spread, 1)
            pe.wait_ge(nl_set, 1)
            values(0)
            for k in range(2 * C):
                if k == 0:
                    pe.wait_ge(alpha2_set, 1)
                    pe.wait_ge(signs_set, 1)
                c, n = divmod(k, 2)
                for j in range(4):
                    last = pe.transpose(ps[:, k, tile(j)], sw1[:, 4 * n + j, tile(c)], ident[:])
                last.then_inc(signs_turned, 1)
            pe.wait_ge(sgn1_set, 2)
            scores(0, 0)
            for k in range(J // 2):
                pe.wait_ge(vl_set, k + 1)
                if k == 0:
                    pe.wait_ge(signs_set, 2)
                for j in range(2):
                    for c in range(C):
                        last = pe.transpose(ps[:, 4 + k, j * D + c * P:j * D + (c + 1) * P],
                                            sw2[:, c, tile(2 * k + j)], ident[:])
                last.then_inc(signs_turned, 1)
            pe.wait_ge(sgn2_set, J // 2)

            def batch(i, s, more):
                b = 2 * i + s
                scores(b, 1)
                turn_probs(b, 0)
                for q in range(T - 2):
                    scores(b, q + 2)
                    turn_probs(b, q + 1)
                    weigh_values(b, q)
                if more:
                    turn_rows(b + 1, 0)
                turn_probs(b, T - 1)
                if more:
                    turn_rows(b + 1, 1)
                weigh_values(b, T - 2)
                if not more:
                    last_ffn(b)
                    return
                weigh_values(b, T - 1)
                queries(b + 1, False)
                for n in range(N2):
                    pe.wait_ge(km_set, N2 * (b + 1) + n + 1)
                    turn_rows_ffn(b, n, 2 * n)
                values(b + 1)
                for j in range(J):
                    if j == 0:
                        pe.wait_ge(x2l_set, N2 * (b + 1))
                    if j == 1:
                        pe.wait_ge(vl_set, VG * (b + 1) + 2)
                    if j >= 2:
                        pe.wait_ge(gelu_set, J * b + j - 1)
                    for c in range(C):
                        for part in (x2h, x2l):
                            for n in range(N2):
                                last = pe.matmul(ps[:, 2 + 2 * (j % 2) + n, :], sgn1[:, c, tile(j)], part[:, c, half(n)],
                                                 start=c == 0 and part is x2h, stop=c == C - 1 and part is x2l)
                    last.then_inc(hidden, 1)
                scores(b + 1, 0)
                ffn_rows(b, 0, range(J - 1), True, True)
                ffn_rows(b, 1, range(J // 2), False, True)
                ffn_rows(b, 0, range(J - 1, J), True, True)
                ffn_rows(b, 1, range(J // 2, J), False, True)
                for t in range(2, T):
                    ffn_rows(b, t, range(J), False, True)

            with pe.Fori(0, PAIRS - 1) as i:
                batch(i, 0, True)
                batch(i, 1, True)
            batch(PAIRS - 1, 0, True)
            batch(PAIRS - 1, 1, False)


_INS = ["L0_attn_x", "L0_attn_Wq", "L0_attn_bq", "L0_attn_Wk", "L0_attn_bk", "L0_attn_Wv", "L0_attn_bv",
        "L0_attn_Wo", "L0_attn_bo", "L0_ffn_w1", "L0_ffn_b1", "L0_ffn_w2", "L0_ffn_b2"]


def kernel(**inputs):
    import numpy as _np
    import concourse.bacc as _bacc
    from concourse import mybir as _mybir
    from concourse.bass_utils import run_bass_kernel_spmd as _run

    nc = _bacc.Bacc("TRN2", target_bir_lowering=False, num_devices=1)
    arrays, args = {}, []
    for name in _INS:
        a = _np.ascontiguousarray(inputs[name])
        arrays[f"in_{name}_dram"] = a
        args.append(nc.dram_tensor(f"in_{name}_dram", a.shape, _mybir.dt.from_np(a.dtype), kind="ExternalInput").ap())
    shape = tuple(inputs["L0_attn_x"].shape)
    mask = gaussian_mask_row(shape[1], shape[1] // P)
    arrays["mask_dram"] = mask
    args.append(nc.dram_tensor("mask_dram", mask.shape, _mybir.dt.from_np(mask.dtype), kind="ExternalInput").ap())
    args.append(nc.dram_tensor("out_dram", shape, F32, kind="ExternalOutput").ap())
    preln_attention_ffn(nc, *args)
    r = _run(nc, [arrays], core_ids=[0])
    return r.results[0]["out_dram"]
```
